# Optimizing a Trainium2 kernel written in Bass

```python
import numpy as np
import jax
import jax.numpy as jnp

def _softmax(x, axis=-1):
    return jax.nn.softmax(x, axis=axis)

def _gelu(x):
    return jax.nn.gelu(x, approximate=True)

def _silu(x):
    return jax.nn.silu(x)

def _sigmoid(x):
    return jax.nn.sigmoid(x)

def _layernorm(x, axis=-1, eps=1e-05):
    m = jnp.mean(x, axis=axis, keepdims=True)
    v = jnp.var(x, axis=axis, keepdims=True)
    return (x - m) / jnp.sqrt(v + eps)

def _scatter_add(tgt, idx, src, axis=0):
    return tgt.at[idx].add(src)

def _segment_sum(src, seg, n):
    return jax.ops.segment_sum(src, seg, n)
kernel_name = 'mk_hybrid_d1_jaxref_r8_a590be'

def setup_inputs(seed: int=0):
    np.random.seed(seed)
    _w = jnp.asarray

    def _L0_attn_a_setup():
        import jax, jax.numpy as jnp
        import numpy as np
        B, T, HID = (1, 128, 256)
        H, DK, DV, M, KW = (16, 128, 128, 128, 4)
        SCALE = DK ** (-0.5)
        EPS = 1e-05

        def short_conv(x, w):
            K = w.shape[1]
            xp = jnp.pad(x, ((0, 0), (K - 1, 0), (0, 0)))
            t = x.shape[1]
            y = sum((xp[:, i:i + t] * w[:, i] for i in range(K)))
            return jax.nn.silu(y)

        def l2norm(x):
            return x * jax.lax.rsqrt(jnp.sum(x * x, axis=-1, keepdims=True) + 1e-06)

        def gsa2_scan(q, k, v, w, g, beta):
            b = q.shape[0]
            tm = lambda x: jnp.moveaxis(x, 1, 0)
            Sk0 = jnp.zeros((b, H, DK, M), q.dtype)
            Sv0 = jnp.zeros((b, H, M, DV), q.dtype)

            def step(carry, xs):
                Sk, Sv = carry
                q_t, k_t, v_t, w_t, g_t, b_t = xs
                gt = jnp.exp(g_t)
                bw = b_t[:, :, None] * w_t
                Sk = Sk * gt[:, :, None, :] + k_t[..., :, None] * bw[:, :, None, :]
                Sv = Sv * gt[..., None] + bw[..., None] * v_t[:, :, None, :]
                s = jnp.einsum('bhd,bhdm->bhm', q_t, Sk) * SCALE
                a = jax.nn.softmax(s, axis=-1)
                o_t = jnp.einsum('bhm,bhmd->bhd', a, Sv)
                return ((Sk, Sv), o_t)
            (_, _), o = jax.lax.scan(step, (Sk0, Sv0), (tm(q), tm(k), tm(v), tm(w), tm(g), tm(beta)))
            return jnp.moveaxis(o, 0, 1)
        key = jax.random.key(seed)
        ks = jax.random.split(key, 16)
        s = 0.02
        return {'hidden_states': jax.random.normal(ks[0], (B, T, HID), jnp.float32), 'Wq': jax.random.normal(ks[1], (HID, H * DK), jnp.float32) * s, 'Wk': jax.random.normal(ks[2], (HID, H * DK), jnp.float32) * s, 'Wv': jax.random.normal(ks[3], (HID, H * DV), jnp.float32) * s, 'Ww': jax.random.normal(ks[4], (HID, H * M), jnp.float32) * s, 'cq': jax.random.normal(ks[5], (H * DK, KW), jnp.float32) * 0.2, 'ck': jax.random.normal(ks[6], (H * DK, KW), jnp.float32) * 0.2, 'cv': jax.random.normal(ks[7], (H * DV, KW), jnp.float32) * 0.2, 'Wf1': jax.random.normal(ks[8], (HID, DV), jnp.float32) * s, 'Wf2': jax.random.normal(ks[9], (DV, H * M), jnp.float32) * s, 'Wb': jax.random.normal(ks[10], (HID, H), jnp.float32) * s, 'Wg1': jax.random.normal(ks[11], (HID, DV), jnp.float32) * s, 'Wg2': jax.random.normal(ks[12], (DV, H * DV), jnp.float32) * s, 'bg2': jnp.zeros((H * DV,), jnp.float32), 'norm_w': jnp.ones((DV,), jnp.float32), 'Wo': jax.random.normal(ks[13], (H * DV, HID), jnp.float32) * s}
    _L0_attn_a_in = _L0_attn_a_setup()

    def _L0_attn_b_setup():
        import jax, jax.numpy as jnp
        import numpy as np
        D_MODEL = 256
        HEAD_SIZE = 64
        N_HEAD = D_MODEL // HEAD_SIZE
        B, T = (2, 128)

        def _layernorm(x, gamma, beta, eps=1e-05):
            mu = jnp.mean(x, axis=-1, keepdims=True)
            var = jnp.var(x, axis=-1, keepdims=True)
            return (x - mu) * jax.lax.rsqrt(var + eps) * gamma + beta

        def _reference_tuple_inner(x, Wx, Ww, bw, Wk, Wv, Wr, Wout, gamma, beta):
            b, t, c = x.shape
            h, n = (N_HEAD, HEAD_SIZE)
            xn = _layernorm(x, gamma, beta)
            w = jax.nn.sigmoid(jnp.einsum('btc,cd->btd', jnp.einsum('btc,cd->btd', xn, Wx), Ww) + bw)
            k = jnp.einsum('btc,cd->btd', xn, Wk)
            v = jnp.einsum('btc,cd->btd', xn, Wv)
            r = jax.nn.sigmoid(jnp.einsum('btc,cd->btd', xn, Wr))

            def tm(a):
                return a.reshape(b, t, h, n).transpose(1, 0, 2, 3)
            k, v, w, r = (tm(k), tm(v), tm(w), tm(r))
            state0 = jnp.zeros((b, h, n, n), x.dtype)

            def step(state, inp):
                k_t, v_t, w_t, r_t = inp
                kv = k_t[..., :, None] * v_t[..., None, :]
                state = (1.0 - w_t)[..., :, None] * state + kv
                y_t = jnp.einsum('bhi,bhij->bhj', r_t, state)
                return (state, y_t)
            state, ys = jax.lax.scan(step, state0, (k, v, w, r))
            y = ys.transpose(1, 0, 2, 3).reshape(b, t, c)
            out = jnp.einsum('btc,cd->btd', y, Wout)
            return (out, state)
        key = jax.random.key(seed)
        ks = jax.random.split(key, 8)
        s = 1.0 / np.sqrt(D_MODEL)
        return {'x': jax.random.normal(ks[0], (B, T, D_MODEL), jnp.float32), 'Wx': jax.random.normal(ks[1], (D_MODEL, D_MODEL), jnp.float32) * s, 'Ww': jax.random.normal(ks[2], (D_MODEL, D_MODEL), jnp.float32) * s, 'bw': jnp.zeros((D_MODEL,), jnp.float32), 'Wk': jax.random.normal(ks[3], (D_MODEL, D_MODEL), jnp.float32) * s, 'Wv': jax.random.normal(ks[4], (D_MODEL, D_MODEL), jnp.float32) * s, 'Wr': jax.random.normal(ks[5], (D_MODEL, D_MODEL), jnp.float32) * s, 'Wout': jax.random.normal(ks[6], (D_MODEL, D_MODEL), jnp.float32) * s, 'gamma': jnp.ones((D_MODEL,), jnp.float32), 'beta': jnp.zeros((D_MODEL,), jnp.float32)}
    _L0_attn_b_in = _L0_attn_b_setup()

    def _L0_ffn_setup():
        import jax, jax.numpy as jnp
        import numpy as np
        TOPK = 6
        CAP = 128
        ROUTE_SCALE = 1.0
        key = jax.random.key(seed)
        k = jax.random.split(key, 6)
        B, T, C = (2, 256, 256)
        E, H, HS = (64, 32, 64)
        std = 0.01
        return {'x': jax.random.normal(k[0], (B, T, C), jnp.float32), 'w_gate': jax.random.normal(k[1], (C, E), jnp.float32) * std, 'w_shared_up': jax.random.normal(k[2], (C, 2 * HS), jnp.float32) * std, 'w_shared_down': jax.random.normal(k[3], (HS, C), jnp.float32) * std, 'w_up': jax.random.normal(k[4], (E, C, 2 * H), jnp.float32) * std, 'w_down': jax.random.normal(k[5], (E, H, C), jnp.float32) * std}
    _L0_ffn_in = _L0_ffn_setup()
    _d = {'L0_attn_a_hidden_states': _L0_attn_a_in['hidden_states'], 'L0_attn_a_Wq': _L0_attn_a_in['Wq'], 'L0_attn_a_Wk': _L0_attn_a_in['Wk'], 'L0_attn_a_Wv': _L0_attn_a_in['Wv'], 'L0_attn_a_Ww': _L0_attn_a_in['Ww'], 'L0_attn_a_cq': _L0_attn_a_in['cq'], 'L0_attn_a_ck': _L0_attn_a_in['ck'], 'L0_attn_a_cv': _L0_attn_a_in['cv'], 'L0_attn_a_Wf1': _L0_attn_a_in['Wf1'], 'L0_attn_a_Wf2': _L0_attn_a_in['Wf2'], 'L0_attn_a_Wb': _L0_attn_a_in['Wb'], 'L0_attn_a_Wg1': _L0_attn_a_in['Wg1'], 'L0_attn_a_Wg2': _L0_attn_a_in['Wg2'], 'L0_attn_a_bg2': _L0_attn_a_in['bg2'], 'L0_attn_a_norm_w': _L0_attn_a_in['norm_w'], 'L0_attn_a_Wo': _L0_attn_a_in['Wo'], 'L0_attn_b_Wx': _L0_attn_b_in['Wx'], 'L0_attn_b_Ww': _L0_attn_b_in['Ww'], 'L0_attn_b_bw': _L0_attn_b_in['bw'], 'L0_attn_b_Wk': _L0_attn_b_in['Wk'], 'L0_attn_b_Wv': _L0_attn_b_in['Wv'], 'L0_attn_b_Wr': _L0_attn_b_in['Wr'], 'L0_attn_b_Wout': _L0_attn_b_in['Wout'], 'L0_attn_b_gamma': _L0_attn_b_in['gamma'], 'L0_attn_b_beta': _L0_attn_b_in['beta'], 'L0_ffn_w_gate': _L0_ffn_in['w_gate'], 'L0_ffn_w_shared_up': _L0_ffn_in['w_shared_up'], 'L0_ffn_w_shared_down': _L0_ffn_in['w_shared_down'], 'L0_ffn_w_up': _L0_ffn_in['w_up'], 'L0_ffn_w_down': _L0_ffn_in['w_down']}
    _x0 = _d['L0_attn_a_hidden_states']
    _d['L0_attn_a_hidden_states'] = jax.random.normal(jax.random.fold_in(jax.random.key(seed), 1), (2, 512, 256), dtype=_x0.dtype)
    del _x0
    return _d

def reference(L0_attn_a_hidden_states, L0_attn_a_Wq, L0_attn_a_Wk, L0_attn_a_Wv, L0_attn_a_Ww, L0_attn_a_cq, L0_attn_a_ck, L0_attn_a_cv, L0_attn_a_Wf1, L0_attn_a_Wf2, L0_attn_a_Wb, L0_attn_a_Wg1, L0_attn_a_Wg2, L0_attn_a_bg2, L0_attn_a_norm_w, L0_attn_a_Wo, L0_attn_b_Wx, L0_attn_b_Ww, L0_attn_b_bw, L0_attn_b_Wk, L0_attn_b_Wv, L0_attn_b_Wr, L0_attn_b_Wout, L0_attn_b_gamma, L0_attn_b_beta, L0_ffn_w_gate, L0_ffn_w_shared_up, L0_ffn_w_shared_down, L0_ffn_w_up, L0_ffn_w_down):

    def _L0_attn_a_ref(hidden_states, Wq, Wk, Wv, Ww, cq, ck, cv, Wf1, Wf2, Wb, Wg1, Wg2, bg2, norm_w, Wo):
        import jax, jax.numpy as jnp
        import numpy as np
        B, T, HID = (1, 128, 256)
        H, DK, DV, M, KW = (16, 128, 128, 128, 4)
        SCALE = DK ** (-0.5)
        EPS = 1e-05

        def short_conv(x, w):
            K = w.shape[1]
            xp = jnp.pad(x, ((0, 0), (K - 1, 0), (0, 0)))
            t = x.shape[1]
            y = sum((xp[:, i:i + t] * w[:, i] for i in range(K)))
            return jax.nn.silu(y)

        def l2norm(x):
            return x * jax.lax.rsqrt(jnp.sum(x * x, axis=-1, keepdims=True) + 1e-06)

        def gsa2_scan(q, k, v, w, g, beta):
            b = q.shape[0]
            tm = lambda x: jnp.moveaxis(x, 1, 0)
            Sk0 = jnp.zeros((b, H, DK, M), q.dtype)
            Sv0 = jnp.zeros((b, H, M, DV), q.dtype)

            def step(carry, xs):
                Sk, Sv = carry
                q_t, k_t, v_t, w_t, g_t, b_t = xs
                gt = jnp.exp(g_t)
                bw = b_t[:, :, None] * w_t
                Sk = Sk * gt[:, :, None, :] + k_t[..., :, None] * bw[:, :, None, :]
                Sv = Sv * gt[..., None] + bw[..., None] * v_t[:, :, None, :]
                s = jnp.einsum('bhd,bhdm->bhm', q_t, Sk) * SCALE
                a = jax.nn.softmax(s, axis=-1)
                o_t = jnp.einsum('bhm,bhmd->bhd', a, Sv)
                return ((Sk, Sv), o_t)
            (_, _), o = jax.lax.scan(step, (Sk0, Sv0), (tm(q), tm(k), tm(v), tm(w), tm(g), tm(beta)))
            return jnp.moveaxis(o, 0, 1)
        h = hidden_states
        q = short_conv(h @ Wq, cq)
        k = short_conv(h @ Wk, ck)
        v = short_conv(h @ Wv, cv)
        w = short_conv(h @ Ww, cv)
        g = jax.nn.log_sigmoid(h @ Wf1 @ Wf2)
        beta = jax.nn.sigmoid(h @ Wb)
        rs = lambda x, d: x.reshape(x.shape[0], x.shape[1], -1, d)
        q, k = (rs(q, DK), rs(k, DK))
        v = rs(v, DV)
        w = l2norm(rs(w, M))
        g = rs(g, M)
        o = gsa2_scan(q, k, v, w, g, beta)
        gate = rs(h @ Wg1 @ Wg2 + bg2, DV)
        o = o * jax.lax.rsqrt(jnp.mean(o * o, axis=-1, keepdims=True) + EPS)
        o = o * norm_w * jax.nn.sigmoid(gate)
        o = o.reshape(o.shape[0], o.shape[1], -1)
        return o @ Wo

    def _L0_attn_b_ref(x, Wx, Ww, bw, Wk, Wv, Wr, Wout, gamma, beta):
        import jax, jax.numpy as jnp
        import numpy as np
        D_MODEL = 256
        HEAD_SIZE = 64
        N_HEAD = D_MODEL // HEAD_SIZE
        B, T = (2, 128)

        def _layernorm(x, gamma, beta, eps=1e-05):
            mu = jnp.mean(x, axis=-1, keepdims=True)
            var = jnp.var(x, axis=-1, keepdims=True)
            return (x - mu) * jax.lax.rsqrt(var + eps) * gamma + beta

        def _reference_tuple_inner(x, Wx, Ww, bw, Wk, Wv, Wr, Wout, gamma, beta):
            b, t, c = x.shape
            h, n = (N_HEAD, HEAD_SIZE)
            xn = _layernorm(x, gamma, beta)
            w = jax.nn.sigmoid(jnp.einsum('btc,cd->btd', jnp.einsum('btc,cd->btd', xn, Wx), Ww) + bw)
            k = jnp.einsum('btc,cd->btd', xn, Wk)
            v = jnp.einsum('btc,cd->btd', xn, Wv)
            r = jax.nn.sigmoid(jnp.einsum('btc,cd->btd', xn, Wr))

            def tm(a):
                return a.reshape(b, t, h, n).transpose(1, 0, 2, 3)
            k, v, w, r = (tm(k), tm(v), tm(w), tm(r))
            state0 = jnp.zeros((b, h, n, n), x.dtype)

            def step(state, inp):
                k_t, v_t, w_t, r_t = inp
                kv = k_t[..., :, None] * v_t[..., None, :]
                state = (1.0 - w_t)[..., :, None] * state + kv
                y_t = jnp.einsum('bhi,bhij->bhj', r_t, state)
                return (state, y_t)
            state, ys = jax.lax.scan(step, state0, (k, v, w, r))
            y = ys.transpose(1, 0, 2, 3).reshape(b, t, c)
            out = jnp.einsum('btc,cd->btd', y, Wout)
            return (out, state)
        return _reference_tuple_inner(x, Wx, Ww, bw, Wk, Wv, Wr, Wout, gamma, beta)[0]

    def _L0_ffn_ref(x, w_gate, w_shared_up, w_shared_down, w_up, w_down):
        import jax, jax.numpy as jnp
        import numpy as np
        TOPK = 6
        CAP = 128
        ROUTE_SCALE = 1.0
        B, T, C = x.shape
        E = w_gate.shape[1]
        x_flat = x.reshape(-1, C)
        N = x_flat.shape[0]
        su = x_flat @ w_shared_up
        y_s, g_s = jnp.split(su, 2, axis=-1)
        shared = jax.nn.silu(g_s) * y_s @ w_shared_down
        scores = jax.nn.sigmoid(x_flat @ w_gate)
        _, topk_idx = jax.lax.top_k(scores, TOPK)
        w = jnp.take_along_axis(scores, topk_idx, axis=-1)
        w = w / w.sum(-1, keepdims=True) * ROUTE_SCALE
        flat_e = topk_idx.reshape(-1)
        oh = jax.nn.one_hot(flat_e, E, dtype=jnp.int32)
        pos = jnp.take_along_axis(jnp.cumsum(oh, axis=0), flat_e[:, None], axis=1)[:, 0] - 1
        valid = pos < CAP
        pos_c = jnp.where(valid, pos, CAP - 1)
        token_ids = jnp.repeat(jnp.arange(N), TOPK)
        x_disp = jnp.zeros((E, CAP, C), x.dtype).at[flat_e, pos].set(x_flat[token_ids], mode='drop')
        up = jnp.einsum('ecd,edh->ech', x_disp, w_up)
        g_r, v_r = jnp.split(up, 2, axis=-1)
        h_r = jax.nn.silu(g_r) * v_r
        out_r = jnp.einsum('ech,ehd->ecd', h_r, w_down)
        y_ts = out_r[flat_e, pos_c]
        y_ts = jnp.where(valid[:, None], y_ts, 0.0)
        routed = (y_ts.reshape(N, TOPK, C) * w[:, :, None]).sum(axis=1)
        return (shared + routed).reshape(B, T, C)
    x = L0_attn_a_hidden_states
    x = x + _L0_attn_a_ref(_layernorm(x, axis=-1), L0_attn_a_Wq, L0_attn_a_Wk, L0_attn_a_Wv, L0_attn_a_Ww, L0_attn_a_cq, L0_attn_a_ck, L0_attn_a_cv, L0_attn_a_Wf1, L0_attn_a_Wf2, L0_attn_a_Wb, L0_attn_a_Wg1, L0_attn_a_Wg2, L0_attn_a_bg2, L0_attn_a_norm_w, L0_attn_a_Wo)
    x = x + _L0_ffn_ref(_layernorm(x, axis=-1), L0_ffn_w_gate, L0_ffn_w_shared_up, L0_ffn_w_shared_down, L0_ffn_w_up, L0_ffn_w_down)
    x = x + _L0_attn_b_ref(_layernorm(x, axis=-1), L0_attn_b_Wx, L0_attn_b_Ww, L0_attn_b_bw, L0_attn_b_Wk, L0_attn_b_Wv, L0_attn_b_Wr, L0_attn_b_Wout, L0_attn_b_gamma, L0_attn_b_beta)
    x = x + _L0_ffn_ref(_layernorm(x, axis=-1), L0_ffn_w_gate, L0_ffn_w_shared_up, L0_ffn_w_shared_down, L0_ffn_w_up, L0_ffn_w_down)
    return x

_drawn_inputs = setup_inputs


def setup_inputs(seed=0):
    import zlib

    import numpy as np

    out = dict(_drawn_inputs(seed))
    spreads = {'L0_attn_a_bg2': (0.0, 0.8),
     'L0_attn_a_norm_w': (1.0, 0.6),
     'L0_attn_b_bw': (0.0, 0.1),
     'L0_attn_b_gamma': (1.0, 0.2),
     'L0_attn_b_beta': (0.0, 0.1)}
    factors = {'L0_attn_a_Wq': 8.0,
     'L0_attn_a_Wk': 8.0,
     'L0_attn_a_cq': 8.0,
     'L0_attn_a_ck': 8.0,
     'L0_attn_a_Wf1': 8.0,
     'L0_attn_a_Wf2': 8.0,
     'L0_attn_a_Wb': 5.002,
     'L0_attn_a_Wg1': 8.0,
     'L0_attn_a_Wg2': 8.0,
     'L0_ffn_w_gate': 8.0,
     'L0_ffn_w_shared_up': 8.0,
     'L0_ffn_w_shared_down': 8.0,
     'L0_ffn_w_up': 8.0,
     'L0_ffn_w_down': 8.0}
    for name, (base, spread) in spreads.items():
        noise = np.random.default_rng([zlib.crc32(name.encode()), seed]).standard_normal(out[name].shape)
        drawn = base * np.exp(spread * noise) if base else spread * noise
        out[name] = jnp.asarray(drawn.astype(out[name].dtype))
    for name, factor in factors.items():
        out[name] = (out[name] * factor).astype(out[name].dtype)
    return out
```

```python
from contextlib import ExitStack

import numpy as np

import concourse.bass as bass
from concourse import mybir
from concourse.alu_op_type import AluOpType as ALU

F32 = mybir.dt.float32
U32 = mybir.dt.uint32
I32 = mybir.dt.int32
ACT = mybir.ActivationFunctionType
X = mybir.AxisListType.X
P = 128

B, T, HID = 2, 512, 256
TILES = B * T // P
NC = T // P
KC = HID // P
H, D = 16, 128
KW = 4
SCALE = float(D) ** -0.5
EPS = 1e-5
BH, BD = 4, 64
NE, EH, TOPK, CAP = 64, 32, 6, 128
SH = 64
FLOOR = 20.0
SUB = 8
LEVELS = (8, 16, 32, 64)
NL = len(LEVELS)
BASE, START, END = 0, NL + 1, NL + 2


def constants():
    j, t = np.arange(P)[:, None], np.arange(P)[None, :]
    sums = np.zeros((P, NL + 3, P), np.float32)
    mask = np.zeros((P, NL + 1, P), np.float32)
    mid = t - t % SUB + SUB // 2
    sums[:, BASE] = 1.0 * ((j >= mid) & (j <= t)) - 1.0 * ((j > t) & (j < mid)) - 0.5 * (j == mid)
    mask[:, BASE] = (j // SUB == t // SUB) & (j <= t)
    for n, size in enumerate(LEVELS):
        mid = t - t % (2 * size) + size
        sums[:, n + 1] = ((j >= mid) & (j <= t)) | ((j > t) & (j < mid))
        mask[:, n + 1] = (j // (2 * size) == t // (2 * size)) & (j % (2 * size) < size) & (t % (2 * size) >= size)
    sums[:, START] = j <= t
    sums[:, END] = j > t
    before = (j < t).astype(np.float32)
    return np.concatenate([sums.reshape(P, -1), mask.reshape(P, -1), np.eye(P, dtype=np.float32), before], axis=1)


N_CONST = (NL + 3) * P + (NL + 1) * P + P + P


class Phase:

    def __init__(self, nc, name):
        self.nc, self.name, self.ctx, self.sems = nc, name, ExitStack(), []

    def __enter__(self):
        self.ctx.__enter__()
        return self

    def __exit__(self, *a):
        left = self.ctx.__exit__(*a)
        if self.sems:
            self.nc.clear_and_free_semaphores(self.sems)
        return left

    def sb(self, name, shape, dt=F32):
        return self.ctx.enter_context(self.nc.sbuf_tensor(f"{self.name}_{name}", shape, dt))

    def ps(self, name, shape, dt=F32):
        return self.ctx.enter_context(self.nc.psum_tensor(f"{self.name}_{name}", shape, dt))

    def sem(self, name):
        self.sems.append(self.nc.alloc_semaphore(f"{self.name}_{name}", num=self.nc.free_semaphores[-1]))
        return self.sems[-1]

    def block(self):
        return self.ctx.enter_context(self.nc.Block())


def after(eng, sem, count):
    if not isinstance(count, int) or count > 0:
        eng.wait_ge(sem, count)


def by_tiles(eng, tile):
    for t in range(2):
        tile(t, t)
    with eng.Fori(1, TILES // 2) as i:
        for par in range(2):
            tile(2 * i + par, par)


def layer_norm(nc, name, x, ident, hT, gamma=None, beta=None, loads=()):
    with Phase(nc, name) as ph:
        stats = ph.sb("stats", [P, TILES, 6])
        mv = ph.sb("mv", [P, TILES, 2])
        std = ph.sb("std", [P, TILES])
        rstd = ph.sb("rstd", [P, TILES])
        shift = ph.sb("shift", [P, TILES])
        h = ph.sb("h", [P, TILES, HID])
        eps = ph.sb("eps", [P, 1])
        turned = ph.ps("turned", [P, 4, 512])
        loaded, eps_set, gb_in = ph.sem("loaded"), ph.sem("eps_set"), ph.sem("gb_in")
        stats_done, mv_done, std_done, rstd_done = (ph.sem(s) for s in ("stats_done", "mv_done", "std_done", "rstd_done"))
        shift_done, h_ready, turned_ready, copied = (ph.sem(s) for s in ("shift_done", "h_ready", "turned_ready", "copied"))
        gb = ph.sb("gb", [P, 2, KC])
        blk = ph.block()

        @blk.sync
        def _(sp):
            for dst, src in loads:
                sp.dma_start(dst, src).then_inc(loaded, 16)
            if gamma is not None:
                sp.dma_start(gb[:, 0, :], gamma.rearrange("(k p) -> p k", p=P), allow_slow_non_contiguous=True).then_inc(gb_in, 16)
                sp.dma_start(gb[:, 1, :], beta.rearrange("(k p) -> p k", p=P), allow_slow_non_contiguous=True).then_inc(gb_in, 16)
            if loads:
                sp.wait_ge(loaded, 16 * len(loads))

        @blk.vector
        def _(dve):
            nc.vector.memset(eps[:], EPS).then_inc(eps_set, 1)
            for n in range(TILES):
                nc.vector.bn_stats(stats[:, n, :], x[:, n, :]).then_inc(stats_done, 1)
            for n in range(TILES):
                dve.wait_ge(stats_done, n + 1)
                nc.vector.bn_aggr(mv[:, n, :], stats[:, n, :]).then_inc(mv_done, 1)
            dve.wait_ge(std_done, 1)
            nc.vector.reciprocal(rstd[:], std[:]).then_inc(rstd_done, 1)
            dve.wait_ge(rstd_done, 1)
            nc.vector.scalar_tensor_tensor(shift[:], mv[:, :, 0], -1.0, rstd[:], ALU.mult, ALU.mult).then_inc(shift_done, 1)
            dve.wait_ge(shift_done, 1)
            for n in range(TILES):
                nc.vector.tensor_scalar(h[:, n, :], x[:, n, :], rstd[:, n:n + 1], shift[:, n:n + 1],
                                        ALU.mult, ALU.add).then_inc(h_ready, 1)

        @blk.tensor
        def _(pe):
            for n in range(TILES):
                pe.wait_ge(h_ready, n + 1)
                for k in range(KC):
                    last = nc.tensor.transpose(turned[:, n // 2, (n % 2 + 2 * k) * P:(n % 2 + 2 * k + 1) * P],
                                               h[:, n, k * P:(k + 1) * P], ident)
                last.then_inc(turned_ready, 1)

        @blk.scalar
        def _(act):
            act.wait_ge(mv_done, TILES)
            act.wait_ge(eps_set, 1)
            nc.scalar.activation(std[:], mv[:, :, 1], ACT.Sqrt, bias=eps[:, 0:1]).then_inc(std_done, 1)
            if gamma is not None:
                act.wait_ge(gb_in, 32)
            for pair in range(TILES // 2):
                act.wait_ge(turned_ready, 2 * pair + 2)
                for k in range(KC):
                    dst = hT[:, k, 2 * pair * P:(2 * pair + 2) * P]
                    src = turned[:, pair, 2 * k * P:(2 * k + 2) * P]
                    if gamma is None:
                        nc.scalar.activation(dst, src, ACT.Copy).then_inc(copied, 1)
                    else:
                        nc.scalar.activation(dst, src, ACT.Identity, bias=gb[:, 1, k:k + 1],
                                             scale=gb[:, 0, k:k + 1]).then_inc(copied, 1)
            act.wait_ge(copied, TILES // 2 * KC)


def slot_decays(nc, hT, w, beta_rows, g_dram):
    HF = H * D // 2
    with Phase(nc, "decay") as ph:
        wf1, wb = ph.sb("wf1", [P, KC, D]), ph.sb("wb", [P, KC, H])
        wf2 = ph.sb("wf2", [P, H * D])
        fT = ph.sb("fT", [P, TILES * P])
        away = ph.sb("away", [P, 2, HF])
        e = ph.sb("e", [P, 2, HF])
        ln = ph.sb("ln", [P, 2, HF])
        g = ph.sb("g", [P, 2, HF])
        tb = ph.sb("tb", [P, TILES, H])
        psf = ph.ps("psf", [P, 2, 512])
        psg = ph.ps("psg", [P, 2, HF])
        psb = ph.ps("psb", [P, TILES, H])
        loaded = ph.sem("loaded")
        f_ready, f_copied, b_ready, b_tanh, b_done = (ph.sem(s) for s in ("f_ready", "f_copied", "b_ready", "b_tanh", "b_done"))
        g_raw, g_abs, g_exp, g_ln, g_ready = (ph.sem(s) for s in ("g_raw", "g_abs", "g_exp", "g_ln", "g_ready"))
        g_stored = [ph.sem(f"g_stored{n}") for n in range(2)]
        blk = ph.block()
        halves = 2 * TILES

        @blk.sync
        def _(sp):
            sp.dma_start(wf1[:], w["L0_attn_a_Wf1"].rearrange("(k p) n -> p k n", p=P)).then_inc(loaded, 16)
            sp.dma_start(wb[:], w["L0_attn_a_Wb"].rearrange("(k p) n -> p k n", p=P)).then_inc(loaded, 16)
            sp.dma_start(wf2[:], w["L0_attn_a_Wf2"]).then_inc(loaded, 16)
            for q in range(halves):
                sp.wait_ge(g_ready, q + 1)
                sp.dma_start(g_dram[q % 2 * (H // 2):(q % 2 + 1) * (H // 2), :, q // 2, :].rearrange("h p m -> p h m"),
                             g[:, q % 2, :].rearrange("p (h m) -> p h m", m=D)).then_inc(g_stored[q % 2], 16)
            for n in range(2):
                sp.wait_ge(g_stored[n], 16 * TILES)

        @blk.tensor
        def _(pe):
            pe.wait_ge(loaded, 48)
            for half in range(2):
                for k in range(KC):
                    last = nc.tensor.matmul(psf[:, half, :], wf1[:, k, :], hT[:, k, half * 512:(half + 1) * 512],
                                            start=k == 0, stop=k == KC - 1)
                last.then_inc(f_ready, 1)
            for n in range(TILES):
                for k in range(KC):
                    last = nc.tensor.matmul(psb[:, n, :], hT[:, k, n * P:(n + 1) * P], wb[:, k, :],
                                            start=k == 0, stop=k == KC - 1)
            last.then_inc(b_ready, 1)
            pe.wait_ge(f_copied, 2)
            for q in range(halves):
                if q >= 2:
                    pe.wait_ge(g_ready, q - 1)
                for c in range(HF // 512):
                    last = nc.tensor.matmul(psg[:, q % 2, c * 512:(c + 1) * 512], fT[:, q // 2 * P:(q // 2 + 1) * P],
                                            wf2[:, q % 2 * HF + c * 512:q % 2 * HF + (c + 1) * 512], start=True, stop=True)
                last.then_inc(g_raw, 1)

        @blk.scalar
        def _(act):
            for q in range(halves):
                act.wait_ge(g_raw, q + 1)
                nc.scalar.activation(away[:, q % 2, :], psg[:, q % 2, :], ACT.Abs).then_inc(g_abs, 1)
                act.wait_ge(g_abs, q + 1)
                nc.scalar.activation(e[:, q % 2, :], away[:, q % 2, :], ACT.Exp, scale=-1.0).then_inc(g_exp, 1)
                act.wait_ge(g_exp, q + 1)
                if q >= 2:
                    act.wait_ge(g_ready, q - 1)
                nc.scalar.activation(ln[:, q % 2, :], e[:, q % 2, :], ACT.Ln, bias=1.0).then_inc(g_ln, 1)
            act.wait_ge(b_ready, 1)
            nc.scalar.activation(tb[:], psb[:], ACT.Tanh, scale=0.5).then_inc(b_tanh, 1)

        @blk.vector
        def _(dve):
            for half in range(2):
                dve.wait_ge(f_ready, half + 1)
                nc.vector.tensor_copy(fT[:, half * 512:(half + 1) * 512], psf[:, half, :]).then_inc(f_copied, 1)
            for q in range(halves):
                dve.wait_ge(g_ln, q + 1)
                if q >= 2:
                    dve.wait_ge(g_stored[q % 2], 16 * (q // 2))
                nc.vector.scalar_tensor_tensor(g[:, q % 2, :], psg[:, q % 2, :], 0.0, ln[:, q % 2, :],
                                               ALU.min, ALU.subtract).then_inc(g_ready, 1)
            dve.wait_ge(b_tanh, 1)
            nc.vector.tensor_scalar(beta_rows[:], tb[:], 0.5, 0.5, ALU.mult, ALU.add).then_inc(b_done, 1)
            dve.wait_ge(b_done, 1)


def slot_attention(nc, hT, w, consts, beta_rows, g_dram, o_dram, l_all):
    sums, mask, ident = consts["sums"], consts["mask"], consts["ident"]
    NX = NL + 1
    BT = B * P
    names = ("q", "k", "v", "w")
    order = ("w", "k", "v", "q")
    at_step = {0: (0, 1), 1: (2,), 2: (3,), 3: ()}

    with Phase(nc, "gsa") as ph:
        weights = ph.sb("weights", [P, 2, 4, KC, D])
        taps_all = ph.sb("taps_all", [P, H, 3, KW])
        taps = ph.sb("taps", [P, 2, 3, KW])
        headT = {n: ph.sb(f"{n}T", [P, 2, B, T]) for n in names}
        raw = ph.sb("raw", [P, B, T])
        tanh = ph.sb("tanh", [P, B, T])
        wsq = ph.sb("wsq", [P, B, T])
        ones = ph.sb("ones", [P, 1])
        ss = ph.sb("ss", [P, 3, TILES])
        half3 = ph.sb("half3", [P, 1])
        nwt = ph.sb("nwt", [P, 5, TILES])
        c = ph.sb("c", [P, 2, B, NC])
        g = ph.sb("g", [P, 2, B, NC, D])
        gf = ph.sb("gf", [P, 2, B, NC, D])
        FT = ph.sb("FT", [P, 2, NX + 2, B, P])
        FR = ph.sb("FR", [P, 2, NX + 3, B, P])
        wR = ph.sb("wR", [P, B, D])
        kv = ph.sb("kv", [P, 2, B, 2 * D])
        XT = ph.sb("XT", [P, 2, NX, B, P])
        XR = ph.sb("XR", [P, 2, NX + 1, B, P])
        AM = ph.sb("AM", [P, 2, NX, B, P])
        prod = ph.sb("prod", [P, NX + 1, B, D])
        s_ = ph.sb("s_", [P, B, D])
        negmax = ph.sb("negmax", [P, B])
        bias = ph.sb("bias", [P, B])
        a = ph.sb("a", [P, B, D])
        l = ph.sb("l", [P, 2, B, NC])
        aF = ph.sb("aF", [P, NX + 1, B, P])
        PM = ph.sb("PM", [P, NX, B, P])
        KV = ph.sb("KV", [P, 2, B, 2 * D])
        Sk = ph.sb("Sk", [P, B, D])
        o = ph.sb("o", [P, 2, B, NC, D])
        U = ph.ps("U", [P, NX + 1, B, D])
        V = ph.ps("V", [P, 3, 2, B, D])
        B6 = ph.ps("B6", [P, 2, B, D])
        B7 = ph.ps("B7", [P, 2, B, D])
        Uproj = U[:].rearrange("p x b d -> p (x b d)")
        Vp = V[:].rearrange("p r x b d -> p (r x) b d")

        S = {n: ph.sem(n) for n in (
            "taps_in taps_halved taps_set g_floored ones_set zeros_set half3_set o_out "
            "pe_wk pe_vA pe_z pe_S pe_aT pe_St pe_P pe_SkT pe_O pe_proj pe_ss "
            "act_w act_kv act_z act_a act_Sk act_O act_tap act_tanh act_sq "
            "dve_AM dve_XT dve_XR dve_prod dve_s dve_max dve_bias dve_aF dve_PM dve_KV dve_conv dve_silu dve_ss dve_g1 "
            "pool_c pool_n pool_l").split()}
        blk = ph.block()


        w_in = [ph.sem(f"w_in{n}") for n in range(2)]
        g_in = [ph.sem(f"g_in{n}") for n in range(2)]


        def pe_project(pe, h, hp, p):
            if p == 0:
                pe.wait_ge(w_in[hp], 32 * (h - hp) + 64)
            else:
                after(pe, S["dve_conv"], (KW - 1) * (4 * h + p))
            for half in range(B):
                for k in range(KC):
                    last = nc.tensor.matmul(Uproj[:, half * T:(half + 1) * T], weights[:, hp, names.index(order[p]), k, :],
                                            hT[:, k, half * T:(half + 1) * T], start=k == 0, stop=k == KC - 1)
            last.then_inc(S["pe_proj"], 1)

        def pe_sumsq(pe, h):
            after(pe, S["act_sq"], h + 1)
            for t in range(TILES):
                last = nc.tensor.matmul(Uproj[:, B * T + t:B * T + t + 1], wsq[:, t // NC, t % NC * P:(t % NC + 1) * P],
                                        ones[:], start=True, stop=True)
            last.then_inc(S["pe_ss"], 1)

        def pe_early(pe, eh, en, ep, es, st, prologue):
            tile = slice(en * P, (en + 1) * P)
            after(pe, S["dve_silu"], 4 * (eh + 1))
            if not prologue:
                after(pe, S["act_O"], es - 1)
            for j, name in enumerate(("w", "k")):
                for b in range(B):
                    last = nc.tensor.transpose(B6[:, j, b, :], headT[name][:, ep, b, tile], ident)
            last.then_inc(S["pe_wk"], 1)
            if not prologue:
                after(pe, S["act_Sk"], st)
            for b in range(B):
                nc.tensor.transpose(B7[:, 0, b, :], headT["v"][:, ep, b, tile], ident)
            for b in range(B):
                last = nc.tensor.matmul(B7[:, 1, b, :], headT["k"][:, ep, b, tile], headT["q"][:, ep, b, tile],
                                        start=True, stop=True)
            last.then_inc(S["pe_vA"], 1)
            after(pe, S["g_floored"], eh + 1)
            for z in range(7):
                if z < 3:
                    if not prologue:
                        after(pe, S["dve_PM"], 2 * (es - 1))
                else:
                    after(pe, S["act_z"], 7 * es + z - 2)
                for x in range(2):
                    place = 2 * (z % 3) + x if z < 6 else END
                    if z == 6 and x == 1:
                        break
                    gz = gf if place == BASE else g
                    if z < 3:
                        for b in range(B):
                            last = nc.tensor.matmul(V[:, z % 3, x, b, :], gz[:, ep, b, en, :], sums[:, place, :],
                                                    start=True, stop=True)
                    else:
                        last = nc.tensor.matmul(V[:, z % 3, x, :, :], sums[:, place, :], gz[:, ep, :, en, :],
                                                start=True, stop=True)
                last.then_inc(S["pe_z"], 1)

        def pe_step(pe, h, n, hp, early, last_head):
            s, st = NC * h + n, (NC - 1) * h + n
            e = n % 2
            after(pe, S["dve_XR"], s + 1)
            after(pe, S["dve_prod"], s)
            if n == 0 or not last_head:
                before = sum(len(at_step[m]) for m in range(n))
                after(pe, S["dve_conv"], (KW - 1) * (4 * (h + 1) + before))
                after(pe, S["dve_ss"], h + 1 + (n >= 2))
            for x in range(NX):
                place = x + 1 if x < NL else BASE
                for b in range(B):
                    last = nc.tensor.matmul(U[:, x, b, :], AM[:, e, place, b, :], XR[:, e, place + 1, b, :],
                                            start=True, stop=True)
            if n > 0:
                after(pe, S["act_Sk"], st)
                for b in range(B):
                    last = nc.tensor.matmul(U[:, NX, b, :], headT["q"][:, hp, b, n * P:(n + 1) * P], Sk[:, b, :],
                                            start=True, stop=True)
            last.then_inc(S["pe_S"], 1)
            if early:
                pe_early(pe, *early, False)
            after(pe, S["act_a"], s + 1)
            if early:
                after(pe, S["act_kv"], s + 2)
            for b in range(B):
                last = nc.tensor.transpose(B6[:, 0, b, :], a[:, b, :], ident)
            last.then_inc(S["pe_aT"], 1)
            if n < NC - 1:
                after(pe, S["dve_AM"], s + 2)
                for b in range(B):
                    last = nc.tensor.matmul(B7[:, b, :, :], XR[:, e, 0, b, :], kv[:, e, b, :], start=True, stop=True)
                last.then_inc(S["pe_St"], 1)
            if not last_head:
                after(pe, S["dve_prod"], s + 1)
                for p in at_step[n]:
                    pe_project(pe, h + 1, 1 - hp, p)
                if n == 1:
                    pe_sumsq(pe, h + 1)
            after(pe, S["dve_aF"], s + 1)
            after(pe, S["dve_XT"], s + 1)
            if early:
                after(pe, S["act_z"], 7 * (s + 2))
            for x in range(NX):
                place = x + 1 if x < NL else BASE
                for b in range(B):
                    last = nc.tensor.matmul(Vp[:, x, b, :], XT[:, e, place, b, :], aF[:, x, b, :], start=True, stop=True)
            last.then_inc(S["pe_P"], 1)
            if n < NC - 1:
                after(pe, S["dve_KV"], st + 1)
                for b in range(B):
                    last = nc.tensor.transpose(B7[:, 0, b, :], KV[:, n % 2, b, 0:D], ident)
                last.then_inc(S["pe_SkT"], 1)
            after(pe, S["dve_PM"], 2 * (s + 1))
            for b in range(B):
                for x in range(NX):
                    last = nc.tensor.matmul(B6[:, 0, b, :], PM[:, x, b, :], kv[:, e, b, D:2 * D],
                                            start=x == 0, stop=n == 0 and x == NX - 1)
                if n > 0:
                    last = nc.tensor.matmul(B6[:, 0, b, :], aF[:, NX, b, :], KV[:, (n - 1) % 2, b, D:2 * D],
                                            start=False, stop=True)
            last.then_inc(S["pe_O"], 1)

        def act_piece(act, h, hp, p):
            done = 4 * h + p
            if p == 0:
                after(act, S["taps_set"], h + 1)
            after(act, S["pe_proj"], done + 1)
            after(act, S["dve_silu"], done)
            j = min(names.index(order[p]), 2)
            nc.scalar.activation(raw[:].rearrange("p b t -> p (b t)"), Uproj[:, 0:B * T], ACT.Copy,
                                 scale=taps[:, hp, j, KW - 1:KW]).then_inc(S["act_tap"], 1)
            after(act, S["dve_conv"], (KW - 1) * (done + 1))
            nc.scalar.activation(tanh[:], raw[:], ACT.Tanh).then_inc(S["act_tanh"], 1)
            if p == 0:
                after(act, S["dve_silu"], 4 * h + 1)
                after(act, S["pe_ss"], h)
                nc.scalar.activation(wsq[:], headT["w"][:, hp], ACT.Square).then_inc(S["act_sq"], 1)

        def act_z(act, ee, es, z):
            after(act, S["pe_z"], 7 * es + z + 1)
            F, at = (FT, 0) if z < 3 else (FR, 1)
            if z == 6:
                nc.scalar.activation(FR[:, ee, 0], V[:, 0, 0], ACT.Exp).then_inc(S["act_z"], 1)
                return
            r = z % 3
            if r == 0:
                nc.scalar.activation(F[:, ee, at], V[:, r, 0], ACT.Exp, scale=-1.0)
                nc.scalar.activation(F[:, ee, at + NX], V[:, r, 0], ACT.Exp)
                nc.scalar.activation(F[:, ee, at + 1], V[:, r, 1], ACT.Exp).then_inc(S["act_z"], 1)
            elif r == 1:
                nc.scalar.activation(F[:, ee, at + 2:at + 4], V[:, r], ACT.Exp).then_inc(S["act_z"], 1)
            else:
                nc.scalar.activation(F[:, ee, at + 4], V[:, r, 0], ACT.Exp)
                nc.scalar.activation(F[:, ee, at + NX + 1], V[:, r, 1], ACT.Exp).then_inc(S["act_z"], 1)

        def act_rows(act, eh, en, ep, es, st, prologue):
            ee = en % 2
            after(act, S["pe_wk"], es + 1)
            if not prologue:
                after(act, S["dve_XR"], es)
            nc.scalar.activation(wR[:], B6[:, 0], ACT.Copy).then_inc(S["act_w"], 1)
            after(act, S["pool_c"], eh + 1)
            if not prologue:
                after(act, S["pe_O"], es - 1)
            for b in range(B):
                nc.scalar.activation(kv[:, ee, b, 0:D], B6[:, 1, b, :], ACT.Copy, scale=c[:, ep, b, en:en + 1])
            after(act, S["pe_vA"], es + 1)
            for b in range(B):
                last = nc.scalar.activation(kv[:, ee, b, D:2 * D], B7[:, 0, b, :], ACT.Copy, scale=c[:, ep, b, en:en + 1])
            last.then_inc(S["act_kv"], 1)

        def act_step(act, h, n, hp, early, last_head):
            s, st = NC * h + n, (NC - 1) * h + n
            if early:
                act_rows(act, *early, False)
                for z in range(4):
                    act_z(act, early[1] % 2, early[3], z)
            after(act, S["dve_bias"], s + 1)
            after(act, S["pe_aT"], s)
            if n == 0:
                after(act, S["pool_l"], h)
            for b in range(B):
                last = nc.scalar.activation(a[:, b, :], s_[:, b, :], ACT.Exp, bias=bias[:, b:b + 1], scale=SCALE,
                                            accum_out=l[:, hp, b, n:n + 1])
            last.then_inc(S["act_a"], 1)
            if early:
                for z in range(4, 7):
                    act_z(act, early[1] % 2, early[3], z)
            if not last_head:
                for p in at_step[n]:
                    act_piece(act, h + 1, 1 - hp, p)
            if n < NC - 1:
                after(act, S["pe_SkT"], st + 1)
                nc.scalar.activation(Sk[:], B7[:, 0], ACT.Copy).then_inc(S["act_Sk"], 1)
            after(act, S["pe_O"], s + 1)
            if n == 0:
                after(act, S["o_out"], 16 * h)
            nc.scalar.activation(o[:, hp, :, n, :], B6[:, 0], ACT.Copy).then_inc(S["act_O"], 1)

        def dve_conv(dve, h, hp, p):
            done = 4 * h + p
            j = min(names.index(order[p]), 2)
            after(dve, S["act_tap"], done + 1)
            proj = Uproj[:, 0:B * T].rearrange("p (b t) -> p b t", b=B)
            for back in range(1, KW):
                if back > 1:
                    after(dve, S["dve_conv"], (KW - 1) * done + back - 1)
                nc.vector.scalar_tensor_tensor(raw[:, :, back:T], proj[:, :, 0:T - back],
                                               taps[:, hp, j, KW - 1 - back:KW - back], raw[:, :, back:T],
                                               ALU.mult, ALU.add).then_inc(S["dve_conv"], 1)

        def dve_silu(dve, h, hp, p):
            after(dve, S["act_tanh"], 4 * h + p + 1)
            nc.vector.scalar_tensor_tensor(headT[order[p]][:, hp], tanh[:], 1.0, raw[:], ALU.add, ALU.mult)\
                .then_inc(S["dve_silu"], 1)

        def dve_sumsq(dve, h):
            after(dve, S["pe_ss"], h + 1)
            after(dve, S["pool_c"], h)
            nc.vector.tensor_scalar(ss[:, 0], Uproj[:, B * T:B * T + TILES], 1e-6, None, ALU.add).then_inc(S["dve_g1"], 1)
            after(dve, S["dve_g1"], 3 * h + 1)
            nc.vector.tensor_scalar(ss[:, 1].bitcast(I32), ss[:, 0].bitcast(I32), 1, None,
                                    ALU.logical_shift_right).then_inc(S["dve_g1"], 1)
            nc.vector.tensor_scalar(ss[:, 2], ss[:, 0], -0.5, None, ALU.mult).then_inc(S["dve_g1"], 1)
            after(dve, S["dve_g1"], 3 * h + 3)
            nc.vector.tensor_scalar(nwt[:, 0].bitcast(I32), ss[:, 1].bitcast(I32), -1.0, float(0x5f3759df),
                                    ALU.mult, ALU.add).then_inc(S["dve_ss"], 1)

        def dve_AM(dve, eh, en, ep, es, st):
            ee = en % 2
            after(dve, S["pe_vA"], es + 1)
            after(dve, S["pool_c"], eh + 1)
            after(dve, S["act_kv"], es + 1)
            for b in range(B):
                last = nc.vector.scalar_tensor_tensor(AM[:, ee, :, b, :], B7[:, 1, b, :].unsqueeze(1).broadcast_to([P, NX, P]),
                                                      c[:, ep, b, en:en + 1], mask[:], ALU.mult, ALU.mult)
            last.then_inc(S["dve_AM"], 1)

        def dve_XT(dve, eh, en, ep, es, st):
            ee = en % 2
            after(dve, S["act_z"], 7 * es + 3)
            nc.vector.tensor_tensor(XT[:, ee], FT[:, ee, 0:NX],
                                    headT["w"][:, ep, :, en * P:(en + 1) * P].unsqueeze(1).broadcast_to([P, NX, B, P]),
                                    ALU.mult).then_inc(S["dve_XT"], 1)

        def dve_XR(dve, eh, en, ep, es, st):
            ee = en % 2
            after(dve, S["act_z"], 7 * (es + 1))
            after(dve, S["act_w"], es + 1)
            nc.vector.tensor_tensor(XR[:, ee], FR[:, ee, 0:NX + 1],
                                    wR[:].unsqueeze(1).broadcast_to([P, NX + 1, B, D]), ALU.mult).then_inc(S["dve_XR"], 1)

        def dve_step(dve, h, n, hp, early, last_head):
            s, st = NC * h + n, (NC - 1) * h + n
            e = n % 2
            nx = NX + (n > 0)
            after(dve, S["pe_S"], s + 1)
            nc.vector.tensor_tensor(prod[:, 0:nx], U[:, 0:nx], FR[:, e, 2:2 + nx], ALU.mult).then_inc(S["dve_prod"], 1)
            after(dve, S["dve_prod"], s + 1)
            after(dve, S["act_a"], s)
            nc.vector.tensor_reduce(s_[:].rearrange("p b d -> p (b d)"), prod[:, 0:nx].rearrange("p x b d -> p (b d) x"),
                                    X, ALU.add).then_inc(S["dve_s"], 1)
            after(dve, S["dve_s"], s + 1)
            nc.vector.tensor_reduce(negmax[:], s_[:], X, ALU.max, negate=True).then_inc(S["dve_max"], 1)
            after(dve, S["dve_max"], s + 1)
            nc.vector.tensor_scalar(bias[:], negmax[:], SCALE, None, ALU.mult).then_inc(S["dve_bias"], 1)
            if early:
                dve_AM(dve, *early)
            after(dve, S["pe_aT"], s + 1)
            after(dve, S["pe_O"], s)
            nc.vector.tensor_tensor(aF[:, 0:nx], FT[:, e, 1:1 + nx], B6[:, 0].unsqueeze(1).broadcast_to([P, nx, B, P]),
                                    ALU.mult).then_inc(S["dve_aF"], 1)
            if n < NC - 1:
                after(dve, S["pe_St"], st + 1)
                if n == 0:
                    nc.vector.tensor_copy(KV[:, 0], B7[:].rearrange("p x b d -> p x (b d)")).then_inc(S["dve_KV"], 1)
                else:
                    after(dve, S["dve_KV"], st)
                    for b in range(B):
                        last = nc.vector.scalar_tensor_tensor(KV[:, n % 2, b], KV[:, (n - 1) % 2, b],
                                                              FT[:, e, NX + 1, b, P - 1:P],
                                                              B7[:, b].rearrange("p b d -> p (b d)"), ALU.mult, ALU.add)
                    last.then_inc(S["dve_KV"], 1)
            pieces = () if last_head else at_step[n]
            for p in pieces[0:1]:
                dve_conv(dve, h + 1, 1 - hp, p)
            if early:
                dve_XT(dve, *early)
            for p in pieces[0:1]:
                dve_silu(dve, h + 1, 1 - hp, p)
            for p in pieces[1:2]:
                dve_conv(dve, h + 1, 1 - hp, p)
            if early:
                dve_XR(dve, *early)
            for p in pieces[1:2]:
                dve_silu(dve, h + 1, 1 - hp, p)
            if n == 1 and not last_head:
                dve_sumsq(dve, h + 1)
            if n == 2 and not last_head:
                dve_floor(dve, h + 1, 1 - hp)
            after(dve, S["pe_P"], s + 1)
            nc.vector.tensor_tensor(PM[:, 0:NL], Vp[:, 0:NL],
                                    mask[:, 1:NX].unsqueeze(2).broadcast_to([P, NL, B, P]), ALU.mult).then_inc(S["dve_PM"], 1)
            for b in range(B):
                last = nc.vector.copy_predicated(PM[:, NL, b], mask[:, BASE].bitcast(U32), Vp[:, NL, b])
            last.then_inc(S["dve_PM"], 1)

        def dve_floor(dve, h, hp):
            dve.wait_ge(g_in[hp], 8 * (h - hp) + 16)
            nc.vector.tensor_scalar(gf[:, hp], g[:, hp], -FLOOR, None, ALU.max).then_inc(S["g_floored"], 1)

        def pool_head(pool, h, hp, prologue):
            if not prologue:
                after(pool, S["dve_silu"], 4 * (h - 1))
            nc.gpsimd.tensor_copy(taps[:, hp].unsqueeze(1), taps_all[:, bass.ds(h, 1)]).then_inc(S["taps_set"], 1)

        def pool_newton(pool, h, hp):
            after(pool, S["dve_ss"], h + 1)
            k = 12 * h
            y = nwt[:, 0]
            for it in range(3):
                dst = (nwt[:, 3], nwt[:, 4], nwt[:, 3])[it]
                nc.gpsimd.tensor_tensor(nwt[:, 1], y, y, ALU.mult).then_inc(S["pool_n"], 1)
                after(pool, S["pool_n"], k + 4 * it + 1)
                nc.gpsimd.tensor_tensor(nwt[:, 2], nwt[:, 1], ss[:, 2], ALU.mult).then_inc(S["pool_n"], 1)
                after(pool, S["pool_n"], k + 4 * it + 2)
                nc.gpsimd.tensor_tensor(nwt[:, 1], nwt[:, 2], half3[:].broadcast_to([P, TILES]), ALU.add).then_inc(S["pool_n"], 1)
                after(pool, S["pool_n"], k + 4 * it + 3)
                nc.gpsimd.tensor_tensor(dst, y, nwt[:, 1], ALU.mult).then_inc(S["pool_n"], 1)
                after(pool, S["pool_n"], k + 4 * it + 4)
                y = dst
            nc.gpsimd.tensor_tensor(c[:, hp].rearrange("p b n -> p (b n)").unsqueeze(2), y.unsqueeze(2),
                                    beta_rows[:, :, bass.ds(h, 1)], ALU.mult).then_inc(S["pool_c"], 1)

        def heads(eng, step):
            def pair(i, last_pair):
                for hp in range(2):
                    h = 2 * i + hp
                    last_head = last_pair and hp == 1
                    for n in range(NC):
                        eh, en, ep = (h, n + 1, hp) if n < NC - 1 else (h + 1, 0, 1 - hp)
                        early = (eh, en, ep, NC * h + n + 1, (NC - 1) * h + n)
                        step(eng, h, n, hp, None if last_head and n == NC - 1 else early, last_head)
            pair(0, False)
            with eng.Fori(1, H // 2 - 1) as i:
                pair(i, False)
            pair(H // 2 - 1, True)

        first = (0, 0, 0, 0, 0)

        def load_weights(sp, h, hp):
            for j, name in enumerate(names):
                src = w[f"L0_attn_a_W{name}"].rearrange("(k p) n -> p k n", p=P)[:, :, bass.ds(h * D, D)]
                sp.dma_start(weights[:, hp, j], src).then_inc(w_in[hp], 16)

        def load_g(sp, h, hp):
            sp.dma_start(g[:, hp].rearrange("p b n d -> p (b n d)").unsqueeze(1),
                         g_dram.rearrange("h p t m -> p h (t m)")[:, bass.ds(h, 1)]).then_inc(g_in[hp], 16)

        @blk.sync
        def _(sp):
            for j, name in enumerate(("q", "k", "v")):
                sp.dma_start(taps_all[:, :, j, :], w[f"L0_attn_a_c{name}"].rearrange("(h p) k -> p h k", p=P))\
                    .then_inc(S["taps_in"], 16)
            for h in range(2):
                load_weights(sp, h, h)
            load_g(sp, 0, 0)

            def head(h, hp, weights_too, g_too):
                if weights_too:
                    after(sp, S["pe_proj"], 4 * (h + 1))
                    load_weights(sp, h + 2, hp)
                if g_too:
                    after(sp, S["pe_z"], 7 * NC * h)
                    after(sp, S["g_floored"], h)
                    load_g(sp, h + 1, 1 - hp)
                after(sp, S["act_O"], NC * (h + 1))
                sp.dma_start(o_dram.rearrange("t p c -> p t c")[:, :, bass.ds(h * D, D)],
                             o[:, hp].rearrange("p b n d -> p (b n) d")).then_inc(S["o_out"], 16)
            for hp in range(2):
                head(hp, hp, True, True)
            with sp.Fori(1, H // 2 - 1) as i:
                for hp in range(2):
                    head(2 * i + hp, hp, True, True)
            head(H - 2, 0, False, True)
            head(H - 1, 1, False, False)
            after(sp, S["o_out"], 16 * H)

        @blk.tensor
        def _(pe):
            after(pe, S["ones_set"], 1)
            for p in range(4):
                pe_project(pe, 0, 0, p)
                if p == 1:
                    pe_sumsq(pe, 0)
            pe_early(pe, *first, True)
            heads(pe, pe_step)

        @blk.scalar
        def _(act):
            for p in range(4):
                act_piece(act, 0, 0, p)
            act_rows(act, *first, True)
            for z in range(7):
                act_z(act, 0, 0, z)
            heads(act, act_step)

        @blk.vector
        def _(dve):
            nc.vector.memset(ones[:], 1.0).then_inc(S["ones_set"], 1)
            nc.vector.memset(half3[:], 1.5).then_inc(S["half3_set"], 1)
            nc.vector.memset(PM[:, NL], 0.0).then_inc(S["zeros_set"], 1)
            after(dve, S["taps_in"], 48)
            nc.vector.tensor_scalar(taps_all[:], taps_all[:], 0.5, None, ALU.mult).then_inc(S["taps_halved"], 1)
            for p in range(4):
                dve_conv(dve, 0, 0, p)
                dve_silu(dve, 0, 0, p)
                if p == 1:
                    dve_sumsq(dve, 0)
            dve_floor(dve, 0, 0)
            dve_AM(dve, *first)
            dve_XT(dve, *first)
            dve_XR(dve, *first)
            after(dve, S["zeros_set"], 1)
            heads(dve, dve_step)

        @blk.gpsimd
        def _(pool):
            after(pool, S["taps_halved"], 1)
            after(pool, S["half3_set"], 1)
            pool_head(pool, 0, 0, True)
            pool_newton(pool, 0, 0)

            def head(h, hp, last_head):
                if not last_head:
                    pool_head(pool, h + 1, 1 - hp, False)
                    pool_newton(pool, h + 1, 1 - hp)
                after(pool, S["act_a"], NC * (h + 1))
                nc.gpsimd.tensor_copy(l_all[:, bass.ds(h, 1), :], l[:, hp].rearrange("p b n -> p (b n)").unsqueeze(1))\
                    .then_inc(S["pool_l"], 1)
            for hp in range(2):
                head(hp, hp, False)
            with pool.Fori(1, H // 2 - 1) as i:
                for hp in range(2):
                    head(2 * i + hp, hp, False)
            head(H - 2, 0, False)
            head(H - 1, 1, True)
            after(pool, S["pool_l"], H)


def gated_output(nc, x, hT, w, ident, o_dram, l_all):
    G = 4
    with Phase(nc, "gate") as ph:
        wg1 = ph.sb("wg1", [P, KC, D])
        wg2 = ph.sb("wg2", [P, H * D])
        bg2 = ph.sb("bg2", [1, H * D])
        norm_w = ph.sb("norm_w", [D, 1])
        wo = ph.sb("wo", [D, H, HID])
        ones = ph.sb("ones", [1, P])
        el2 = ph.sb("el2", [P, H, TILES])
        o = ph.sb("o", [P, 2, H, D])
        sq = ph.sb("sq", [P, H, D])
        ss = ph.sb("ss", [P, H])
        ms = ph.sb("ms", [P, H])
        rms = ph.sb("rms", [P, H])
        rrms = ph.sb("rrms", [P, H])
        f = ph.sb("f", [P, 2, P])
        th = ph.sb("th", [P, H, D])
        og = ph.sb("og", [P, H, D])
        y = ph.sb("y", [P, 2, H, D])
        yT = ph.sb("yT", [P, 2, H, P])
        ps_gate = ph.ps("ps_gate", [P, H, D])
        ps_turn = ph.ps("ps_turn", [P, 2, G, P])
        ps_f = ph.ps("ps_f", [P, 512])
        ps_out = ph.ps("ps_out", [P, 512])
        S = {n: ph.sem(n) for n in ("w_in ones_set wo_scaled el2_ready sq ss ms rms rrms f_raw f gate th og y turned "
                                    "yT out x").split()}
        o_in = [ph.sem(f"o_in{n}") for n in range(2)]
        blk = ph.block()

        @blk.sync
        def _(sp):
            sp.dma_start(wg1[:], w["L0_attn_a_Wg1"].rearrange("(k p) n -> p k n", p=P)).then_inc(S["w_in"], 16)
            sp.dma_start(wg2[:], w["L0_attn_a_Wg2"]).then_inc(S["w_in"], 16)
            sp.dma_start(bg2[:], w["L0_attn_a_bg2"].rearrange("(a n) -> a n", a=1)).then_inc(S["w_in"], 16)
            sp.dma_start(norm_w[:], w["L0_attn_a_norm_w"].rearrange("(p a) -> p a", a=1)).then_inc(S["w_in"], 16)
            sp.dma_start(wo[:], w["L0_attn_a_Wo"].rearrange("(h p) n -> p h n", p=P)).then_inc(S["w_in"], 16)

            def tile(t, par):
                after(sp, S["og"], t - 1)
                sp.dma_start(o[:, par].rearrange("p h d -> p (h d)").unsqueeze(1),
                             o_dram.rearrange("t p c -> p t c")[:, bass.ds(t, 1)]).then_inc(o_in[par], 16)
            by_tiles(sp, tile)

        @blk.tensor
        def _(pe):
            pe.wait_ge(S["w_in"], 80)
            pe.wait_ge(S["ones_set"], 1)

            def tile(t, par):
                after(pe, S["f"], t)
                for k in range(KC):
                    last = nc.tensor.matmul(ps_f[:, 0:P], wg1[:, k, :], hT[:, k, bass.ds(t * P, P)],
                                            start=k == 0, stop=k == KC - 1)
                last.then_inc(S["f_raw"], 1)
                pe.wait_ge(S["f"], t + 1)
                after(pe, S["th"], t)
                for q in range(H // G):
                    dst = ps_gate[:, q * G:(q + 1) * G, :]
                    nc.tensor.matmul(dst, f[:, par, :], wg2[:, q * 512:(q + 1) * 512], start=True, stop=False)
                    last = nc.tensor.matmul(dst, ones[:], bg2[:, q * 512:(q + 1) * 512], start=False, stop=True)
                last.then_inc(S["gate"], 1)
                pe.wait_ge(S["y"], t + 1)
                for q in range(H // G):
                    after(pe, S["yT"], H // G * t + q - 1)
                    for j in range(G):
                        last = nc.tensor.transpose(ps_turn[:, q % 2, j, :], y[:, par, q * G + j, :], ident)
                    last.then_inc(S["turned"], 1)
                pe.wait_ge(S["yT"], H // G * (t + 1))
                pe.wait_ge(S["wo_scaled"], 1)
                after(pe, S["x"], t)
                for h in range(H):
                    last = nc.tensor.matmul(ps_out[:, 0:HID], yT[:, par, h, :], wo[:, h, :], start=h == 0, stop=h == H - 1)
                last.then_inc(S["out"], 1)
            by_tiles(pe, tile)

        @blk.scalar
        def _(act):
            def tile(t, par):
                act.wait_ge(S["f_raw"], t + 1)
                nc.scalar.activation(f[:, par], ps_f[:, 0:P], ACT.Copy).then_inc(S["f"], 1)
                act.wait_ge(o_in[par], 8 * (t - par) + 16)
                after(act, S["ss"], t)
                nc.scalar.activation(sq[:], o[:, par], ACT.Square).then_inc(S["sq"], 1)
                act.wait_ge(S["gate"], t + 1)
                after(act, S["og"], t)
                nc.scalar.activation(th[:], ps_gate[:], ACT.Tanh, scale=0.5).then_inc(S["th"], 1)
                act.wait_ge(S["ms"], t + 1)
                nc.scalar.activation(rms[:], ms[:], ACT.Sqrt).then_inc(S["rms"], 1)
                for q in range(H // G):
                    act.wait_ge(S["turned"], H // G * t + q + 1)
                    nc.scalar.activation(yT[:, par, q * G:(q + 1) * G, :], ps_turn[:, q % 2], ACT.Copy).then_inc(S["yT"], 1)
            by_tiles(act, tile)

        @blk.vector
        def _(dve):
            nc.vector.memset(ones[:], 1.0).then_inc(S["ones_set"], 1)
            dve.wait_ge(S["w_in"], 80)
            nc.vector.tensor_scalar(wo[:], wo[:], norm_w[:, 0:1], 0.5, ALU.mult, ALU.mult).then_inc(S["wo_scaled"], 1)
            nc.vector.scalar_tensor_tensor(el2[:], l_all[:], EPS, l_all[:], ALU.mult, ALU.mult).then_inc(S["el2_ready"], 1)
            dve.wait_ge(S["el2_ready"], 1)

            def tile(t, par):
                dve.wait_ge(S["sq"], t + 1)
                nc.vector.tensor_reduce(ss[:], sq[:], X, ALU.add).then_inc(S["ss"], 1)
                dve.wait_ge(S["ss"], t + 1)
                nc.vector.scalar_tensor_tensor(ms[:].unsqueeze(2), ss[:].unsqueeze(2), 1.0 / D, el2[:, :, bass.ds(t, 1)],
                                               ALU.mult, ALU.add).then_inc(S["ms"], 1)
                dve.wait_ge(S["th"], t + 1)
                nc.vector.scalar_tensor_tensor(og[:], th[:], 1.0, o[:, par], ALU.add, ALU.mult).then_inc(S["og"], 1)
                dve.wait_ge(S["rms"], t + 1)
                nc.vector.reciprocal(rrms[:], rms[:]).then_inc(S["rrms"], 1)
                dve.wait_ge(S["rrms"], t + 1)
                after(dve, S["turned"], H // G * (t - 1))
                dve.wait_ge(S["og"], t + 1)
                nc.vector.tensor_tensor(y[:, par], og[:], rrms[:].unsqueeze(2).broadcast_to([P, H, D]), ALU.mult)\
                    .then_inc(S["y"], 1)
                dve.wait_ge(S["out"], t + 1)
                nc.vector.tensor_tensor(x[:, bass.ds(t, 1)], x[:, bass.ds(t, 1)], ps_out[:, 0:HID].unsqueeze(1), ALU.add)\
                    .then_inc(S["x"], 1)
            by_tiles(dve, tile)
            dve.wait_ge(S["x"], TILES)


def experts(nc, name, x, hT, W, consts):
    ident, before = consts["ident"], consts["before"]
    NQ = 4
    EQ = NE // NQ
    CH = NE * EH // P
    CQ = CH // NQ
    with Phase(nc, name) as ph:
        hc = ph.sb("hc", [P, 2, KC, P])
        scores = ph.sb("scores", [P, NE + 2])
        th = ph.sb("th", [P, NE])
        top = ph.sb("top", [P, 8])
        left = ph.sb("left", [P, NE + 2])
        sel = ph.sb("sel", [P, NE])
        seen = ph.sb("seen", [P, NE])
        wsel = ph.sb("wsel", [P, NE])
        wsum = ph.sb("wsum", [P, 1])
        rsum = ph.sb("rsum", [P, 1])
        wcap = ph.sb("wcap", [P, NE])
        comb = ph.sb("comb", [P, 2, NE])
        ones = ph.sb("ones", [P, P])
        ths = ph.sb("ths", [P, SH])
        gs = ph.sb("gs", [P, SH])
        hs = ph.sb("hs", [P, 2, SH])
        hsT = ph.sb("hsT", [SH, 2, P])
        tg = ph.sb("tg", [P, 2, EQ, EH])
        sg = ph.sb("sg", [P, EQ, EH])
        vw = ph.sb("vw", [P, EQ, EH])
        r = ph.sb("r", [P, 2, EQ, EH])
        rT = ph.sb("rT", [P, 2, CH, P])
        ps_up = ph.ps("ps_up", [P, 2, EQ, 2 * EH])
        ps_turn = ph.ps("ps_turn", [P, 2, CQ, P])
        ps_g = ph.ps("ps_g", [P, 512])
        ps_out = ph.ps("ps_out", [P, 512])
        S = {n: ph.sem(n) for n in ("set hc g th ths sc top left sel wsel wsum rsum pos wcap comb seen gs hs up tg sg vw r "
                                    "turned rT hsturned hsT out x").split()}
        blk = ph.block()
        Z, SU, POS = slice(0, NE), slice(NE, NE + 2 * SH), slice(NE + 2 * SH, 2 * NE + 2 * SH)

        @blk.tensor
        def _(pe):
            pe.wait_ge(S["set"], 3)

            def tile(t, par):
                pe.wait_ge(S["hc"], t + 1)
                after(pe, S["hsT"], t)
                for k in range(KC):
                    nc.tensor.matmul(ps_g[:, Z], hc[:, par, k], W["gate"][:, k], start=k == 0, stop=k == KC - 1)
                for k in range(KC):
                    last = nc.tensor.matmul(ps_g[:, SU], hc[:, par, k], W["shared_up"][:, k], start=k == 0, stop=k == KC - 1)
                last.then_inc(S["g"], 1)

                def up(q):
                    after(pe, S["vw"], NQ * t + q - 1)
                    for c in range(2):
                        for k in range(KC):
                            last = nc.tensor.matmul(ps_up[:, q % 2, c * EQ // 2:(c + 1) * EQ // 2, :], hc[:, par, k],
                                                    W["up"][:, k, q * EQ + c * EQ // 2:q * EQ + (c + 1) * EQ // 2, :],
                                                    start=k == 0, stop=k == KC - 1)
                    last.then_inc(S["up"], 1)

                def turn(q):
                    pe.wait_ge(S["r"], NQ * t + q + 1)
                    after(pe, S["rT"], NQ * t + q - 1)
                    for c in range(CQ):
                        last = nc.tensor.transpose(ps_turn[:, q % 2, c, :],
                                                   r[:, q % 2].rearrange("p e h -> p (e h)")[:, c * P:(c + 1) * P], ident)
                    last.then_inc(S["turned"], 1)
                up(0)
                up(1)
                pe.wait_ge(S["seen"], t + 1)
                pe.wait_ge(S["hs"], t + 1)
                nc.tensor.matmul(ps_g[:, POS], before, sel[:], start=True, stop=False)
                nc.tensor.matmul(ps_g[:, POS], ones[:], seen[:], start=False, stop=True).then_inc(S["pos"], 1)
                up(2)
                nc.tensor.transpose(ps_g[0:SH, 2 * NE + 2 * SH:2 * NE + 2 * SH + P], hs[:, par], ident).then_inc(S["hsturned"], 1)
                turn(0)
                up(3)
                turn(1)
                turn(2)
                turn(3)
                pe.wait_ge(S["rT"], NQ * (t + 1))
                pe.wait_ge(S["hsT"], t + 1)
                after(pe, S["x"], t)
                for c in range(CH):
                    nc.tensor.matmul(ps_out[:, 0:HID], rT[:, par, c], W["down"][:, c], start=c == 0, stop=False)
                nc.tensor.matmul(ps_out[:, 0:HID], hsT[:, par], W["shared_down"][:], start=False, stop=True).then_inc(S["out"], 1)
            by_tiles(pe, tile)

        @blk.scalar
        def _(act):
            def tile(t, par):
                after(act, S["out"], t - 1)
                nc.scalar.activation(hc[:, par], hT[:, :, bass.ds(t * P, P)], ACT.Copy).then_inc(S["hc"], 1)
                act.wait_ge(S["g"], t + 1)
                after(act, S["hs"], t)
                nc.scalar.activation(th[:], ps_g[:, Z], ACT.Tanh, scale=0.5).then_inc(S["th"], 1)
                nc.scalar.activation(ths[:], ps_g[:, NE + SH:NE + 2 * SH], ACT.Tanh, scale=0.5).then_inc(S["ths"], 1)

                def tanh_up(q):
                    act.wait_ge(S["up"], NQ * t + q + 1)
                    after(act, S["sg"], NQ * t + q - 1)
                    nc.scalar.activation(tg[:, q % 2], ps_up[:, q % 2, :, 0:EH], ACT.Tanh, scale=0.5).then_inc(S["tg"], 1)

                def copy_r(q):
                    act.wait_ge(S["turned"], NQ * t + q + 1)
                    nc.scalar.activation(rT[:, par, q * CQ:(q + 1) * CQ], ps_turn[:, q % 2], ACT.Copy).then_inc(S["rT"], 1)
                tanh_up(0)
                tanh_up(1)
                act.wait_ge(S["hsturned"], t + 1)
                nc.scalar.activation(hsT[:, par], ps_g[0:SH, 2 * NE + 2 * SH:2 * NE + 2 * SH + P], ACT.Copy).then_inc(S["hsT"], 1)
                tanh_up(2)
                copy_r(0)
                tanh_up(3)
                for q in range(1, NQ):
                    copy_r(q)
            by_tiles(act, tile)

        @blk.vector
        def _(dve):
            nc.vector.memset(ones[:], 1.0).then_inc(S["set"], 1)
            nc.vector.memset(seen[:], 0.0).then_inc(S["set"], 1)
            nc.vector.memset(scores[:, NE:NE + 2], 2.0).then_inc(S["set"], 1)
            dve.wait_ge(S["set"], 3)

            def tile(t, par):
                dve.wait_ge(S["th"], t + 1)
                nc.vector.tensor_scalar(scores[:, 0:NE], th[:], 0.5, 0.5, ALU.mult, ALU.add).then_inc(S["sc"], 1)
                dve.wait_ge(S["sc"], t + 1)
                if isinstance(t, int) and t == 0:
                    pass
                else:
                    dve.wait_ge(S["pos"], t)
                    nc.vector.tensor_tensor(seen[:], seen[:], sel[:], ALU.add)
                nc.vector.max(top[:], scores[:]).then_inc(S["top"], 1)
                dve.wait_ge(S["ths"], t + 1)
                dve.wait_ge(S["top"], t + 1)
                nc.vector.scalar_tensor_tensor(gs[:], ths[:], 1.0, ps_g[:, NE + SH:NE + 2 * SH], ALU.add, ALU.mult)\
                    .then_inc(S["gs"], 1)
                nc.vector.match_replace(left[:], top[:], scores[:], -1.0).then_inc(S["left"], 1)
                dve.wait_ge(S["left"], t + 1)
                nc.vector.tensor_scalar(sel[:], left[:, 0:NE], 0.0, None, ALU.is_lt).then_inc(S["seen"], 1)
                dve.wait_ge(S["seen"], t + 1)
                nc.vector.tensor_tensor(wsel[:], sel[:], scores[:, 0:NE], ALU.mult).then_inc(S["wsel"], 1)
                dve.wait_ge(S["wsel"], t + 1)
                nc.vector.tensor_reduce(wsum[:], wsel[:], X, ALU.add).then_inc(S["wsum"], 1)
                dve.wait_ge(S["gs"], t + 1)
                nc.vector.scalar_tensor_tensor(hs[:, par], gs[:], 0.5, ps_g[:, NE:NE + SH], ALU.mult, ALU.mult)\
                    .then_inc(S["hs"], 1)
                dve.wait_ge(S["wsum"], t + 1)
                nc.vector.reciprocal(rsum[:], wsum[:]).then_inc(S["rsum"], 1)
                dve.wait_ge(S["pos"], t + 1)
                nc.vector.scalar_tensor_tensor(wcap[:], ps_g[:, POS], float(CAP), wsel[:], ALU.is_lt, ALU.mult)\
                    .then_inc(S["wcap"], 1)
                dve.wait_ge(S["wcap"], t + 1)
                dve.wait_ge(S["rsum"], t + 1)
                nc.vector.tensor_scalar(comb[:, par], wcap[:], rsum[:, 0:1], 0.5, ALU.mult, ALU.mult).then_inc(S["comb"], 1)
                dve.wait_ge(S["comb"], t + 1)
                for q in range(NQ):
                    after(dve, S["r"], NQ * t + q)
                    dve.wait_ge(S["tg"], NQ * t + q + 1)
                    nc.vector.scalar_tensor_tensor(sg[:], tg[:, q % 2], 1.0, ps_up[:, q % 2, :, 0:EH], ALU.add, ALU.mult)\
                        .then_inc(S["sg"], 1)
                    nc.vector.tensor_tensor(vw[:], ps_up[:, q % 2, :, EH:2 * EH],
                                            comb[:, par, q * EQ:(q + 1) * EQ].unsqueeze(2).broadcast_to([P, EQ, EH]),
                                            ALU.mult).then_inc(S["vw"], 1)
                    after(dve, S["turned"], NQ * t + q - 1)
                    dve.wait_ge(S["vw"], NQ * t + q + 1)
                    nc.vector.tensor_tensor(r[:, q % 2], sg[:], vw[:], ALU.mult).then_inc(S["r"], 1)
                dve.wait_ge(S["out"], t + 1)
                nc.vector.tensor_tensor(x[:, bass.ds(t, 1)], x[:, bass.ds(t, 1)], ps_out[:, 0:HID].unsqueeze(1), ALU.add)\
                    .then_inc(S["x"], 1)
            by_tiles(dve, tile)
            dve.wait_ge(S["x"], TILES)


def linear_attention(nc, x, hT, w, consts):
    C = BH * BD
    with Phase(nc, "lin") as keep:
        wout = keep.sb("wout", [P, KC, C])
        kT = keep.sb("kT", [P, KC, TILES * P])
        rT = keep.sb("rT", [P, KC, TILES * P])
        kv = keep.sb("kv", [P, TILES, 2, C])
        g = keep.sb("g", [P, TILES, C])
        gf = keep.sb("gf", [P, TILES, C])
        ps = keep.ps("ps", [P, 8, 512])
        linear_inputs(nc, hT, w, wout, kT, rT, kv, g, gf, ps)
        linear_chunks(nc, x, wout, kT, rT, kv, g, gf, ps, consts)


def linear_inputs(nc, hT, w, wout, kT, rT, kv, g, gf, ps):
    C = BH * BD
    with Phase(nc, "lin_in") as ph:
        W = {n: ph.sb(f"W{n}", [P, KC, C]) for n in ("x", "w", "r", "k")} | {"out": wout}
        Wkv = ph.sb("Wkv", [P, KC, 2, C])
        bw = ph.sb("bw", [1, C])
        ones = ph.sb("ones", [1, P])
        uT = ph.sb("uT", [P, KC, TILES * P])
        rth = ph.sb("rth", [P, KC, TILES * P])
        ab = ph.sb("ab", [P, TILES, C])
        ex = ph.sb("ex", [P, TILES, C])
        ln = ph.sb("ln", [P, TILES, C])
        S = {n: ph.sem(n) for n in "w_in ones_set pu u pk pr k rth r pkv kv pz ab ex ln gz g gf".split()}
        blk = ph.block()
        NH = TILES * P // 512

        @blk.sync
        def _(sp):
            for n in ("x", "w", "r", "k", "out"):
                sp.dma_start(W[n][:], w[f"L0_attn_b_W{n}"].rearrange("(k p) n -> p k n", p=P)).then_inc(S["w_in"], 16)
            for j, n in enumerate(("k", "v")):
                sp.dma_start(Wkv[:, :, j], w[f"L0_attn_b_W{n}"].rearrange("(k p) n -> p k n", p=P)).then_inc(S["w_in"], 16)
            sp.dma_start(bw[:], w["L0_attn_b_bw"].rearrange("(a n) -> a n", a=1)).then_inc(S["w_in"], 16)

        def project(weight, first_bank):
            for half in range(KC):
                for c in range(NH):
                    for k in range(KC):
                        last = nc.tensor.matmul(ps[:, first_bank + half * NH + c], weight[:, k, half * P:(half + 1) * P],
                                                hT[:, k, c * 512:(c + 1) * 512], start=k == 0, stop=k == KC - 1)
            return last

        def banks(first):
            return ps[:, first:first + KC * NH].rearrange("p (k c) t -> p k (c t)", k=KC)

        @blk.tensor
        def _(pe):
            pe.wait_ge(S["w_in"], 128)
            pe.wait_ge(S["ones_set"], 1)
            project(W["x"], 0).then_inc(S["pu"], 1)
            project(W["k"], 4).then_inc(S["pk"], 1)
            pe.wait_ge(S["u"], 1)
            for t in range(TILES):
                dst = ps[:, t // 2, t % 2 * C:(t % 2 + 1) * C]
                for k in range(KC):
                    nc.tensor.matmul(dst, uT[:, k, t * P:(t + 1) * P], W["w"][:, k], start=k == 0, stop=False)
                last = nc.tensor.matmul(dst, ones[:], bw[:], start=False, stop=True)
            last.then_inc(S["pz"], 1)
            pe.wait_ge(S["k"], 1)
            project(W["r"], 4).then_inc(S["pr"], 1)
            pe.wait_ge(S["gz"], 1)
            for t in range(TILES):
                if t == 4:
                    pe.wait_ge(S["rth"], 1)
                for k in range(KC):
                    last = nc.tensor.matmul(ps[:, t], hT[:, k, t * P:(t + 1) * P], Wkv[:, k], start=k == 0, stop=k == KC - 1)
                last.then_inc(S["pkv"], 1)

        @blk.scalar
        def _(act):
            act.wait_ge(S["pu"], 1)
            nc.scalar.activation(uT[:], banks(0), ACT.Copy).then_inc(S["u"], 1)
            act.wait_ge(S["pz"], 1)
            z = ps[:, 0:4].rearrange("p a (b c) -> p (a b) c", b=2)
            nc.scalar.activation(ab[:], z, ACT.Abs).then_inc(S["ab"], 1)
            act.wait_ge(S["ab"], 1)
            nc.scalar.activation(ex[:], ab[:], ACT.Exp, scale=-1.0).then_inc(S["ex"], 1)
            act.wait_ge(S["ex"], 1)
            nc.scalar.activation(ln[:], ex[:], ACT.Ln, bias=1.0).then_inc(S["ln"], 1)
            act.wait_ge(S["pr"], 1)
            nc.scalar.activation(rth[:], banks(4), ACT.Tanh, scale=0.5).then_inc(S["rth"], 1)
            for t in range(TILES):
                act.wait_ge(S["pkv"], t + 1)
                nc.scalar.activation(kv[:, t], ps[:, t].rearrange("p (j c) -> p j c", j=2), ACT.Copy).then_inc(S["kv"], 1)
            act.wait_ge(S["kv"], TILES)

        @blk.vector
        def _(dve):
            nc.vector.memset(ones[:], 1.0).then_inc(S["ones_set"], 1)
            dve.wait_ge(S["pk"], 1)
            nc.vector.tensor_copy(kT[:], banks(4)).then_inc(S["k"], 1)
            dve.wait_ge(S["ln"], 1)
            z = ps[:, 0:4].rearrange("p a (b c) -> p (a b c)", b=2)
            nc.vector.scalar_tensor_tensor(ab[:].rearrange("p t c -> p (t c)"), z, 0.0, ln[:].rearrange("p t c -> p (t c)"),
                                           ALU.max, ALU.add).then_inc(S["gz"], 1)
            dve.wait_ge(S["gz"], 1)
            nc.vector.tensor_scalar(g[:], ab[:], -1.0, None, ALU.mult).then_inc(S["g"], 1)
            nc.vector.tensor_scalar(gf[:], ab[:], -1.0, -FLOOR, ALU.mult, ALU.max).then_inc(S["gf"], 1)
            dve.wait_ge(S["rth"], 1)
            nc.vector.tensor_scalar(rT[:], rth[:], 0.5, 0.5, ALU.mult, ALU.add).then_inc(S["r"], 1)
            dve.wait_ge(S["r"], 1)
            dve.wait_ge(S["g"], 1)
            dve.wait_ge(S["gf"], 1)


def linear_chunks(nc, x, wout, kT, rT, kv, g, gf, ps, consts):
    sums, mask, ident = consts["sums"], consts["mask"], consts["ident"]
    NX = NL + 1
    C = BH * BD
    RING = 6
    UNITS = NX * 2
    with Phase(nc, "chunks") as ph:
        F = ph.sb("F", [P, NX + 2, KC, B, P])
        Fend = ph.sb("Fend", [P, B, C])
        XT = ph.sb("XT", [P, NX, KC, B, P])
        EF = ph.sb("EF", [P, NX + 1, KC, B, P])
        Xend = ph.sb("Xend", [P, 2, B, C])
        PM = ph.sb("PM", [P, NX, 2, KC, B, P])
        St = ph.sb("St", [P, 2, KC, B, P])
        y = ph.sb("y", [P, B, C])
        yT = ph.sb("yT", [P, B, KC, P])
        S = {n: ph.sem(n) for n in "zero z F XT EF Xend P PM st St o y yt yT out x".split()}
        blk = ph.block()
        bank_o, bank_s = ps[:, 6], ps[:, 7]

        def kT_of(T_, n):
            return T_[:].rearrange("p k (b t) -> p k b t", b=B)[:, :, :, n * P:(n + 1) * P]

        @blk.tensor
        def _(pe):
            pe.wait_ge(S["zero"], 2)
            for n in range(NC):
                if n:
                    pe.wait_ge(S["PM"], UNITS * n)
                    pe.wait_ge(S["yT"], n)
                for z in range(NX + 1):
                    gz = gf if z == BASE else g
                    for k in range(KC):
                        for b in range(B):
                            last = nc.tensor.matmul(ps[:, z, (k * B + b) * P:(k * B + b + 1) * P],
                                                    gz[:, b * NC + n, k * P:(k + 1) * P], sums[:, z], start=True, stop=True)
                    last.then_inc(S["z"], 1)
                if n:
                    pe.wait_ge(S["y"], n)
                for b in range(B):
                    last = nc.tensor.matmul(bank_o[:, b * C:(b + 1) * C], sums[:, END], g[:, b * NC + n], start=True, stop=True)
                last.then_inc(S["z"], 1)
                if n < NC - 1:
                    pe.wait_ge(S["Xend"], n + 1)
                    if n:
                        pe.wait_ge(S["x"], 2 * n)
                    for k in range(KC):
                        for b in range(B):
                            last = nc.tensor.matmul(bank_s[:, (k * B + b) * P:(k * B + b + 1) * P],
                                                    Xend[:, n % 2, b, k * P:(k + 1) * P],
                                                    kv[:, b * NC + n, 1, k * P:(k + 1) * P], start=True, stop=True)
                    last.then_inc(S["st"], 1)
                pe.wait_ge(S["EF"], n + 1)
                pe.wait_ge(S["F"], (NX + 2) * (n + 1))
                for u in range(UNITS):
                    xl, half = u // 2, u % 2
                    at = half * BD
                    place = xl + 1 if xl < NL else BASE
                    if u >= RING:
                        pe.wait_ge(S["PM"], UNITS * n + u - RING + 1)
                    for k in range(KC):
                        for b in range(B):
                            last = nc.tensor.matmul(ps[:, u % RING, (k * B + b) * P:(k * B + b + 1) * P],
                                                    XT[at:at + BD, place, k, b], EF[at:at + BD, xl, k, b],
                                                    start=True, stop=True)
                    last.then_inc(S["P"], 1)
                pe.wait_ge(S["PM"], UNITS * (n + 1))
                for b in range(B):
                    for k in range(KC):
                        dst = bank_o[:, b * C + k * P:b * C + (k + 1) * P]
                        if n:
                            nc.tensor.matmul(dst, EF[:, NX, k, b], St[:, (n - 1) % 2, k, b], start=True, stop=False)
                        for half in range(2):
                            for xl in range(NX):
                                last = nc.tensor.matmul(dst[:, half * BD:(half + 1) * BD], PM[:, xl, half, k, b],
                                                        kv[:, b * NC + n, 1, k * P + half * BD:k * P + (half + 1) * BD],
                                                        start=n == 0 and xl == 0,
                                                        stop=xl == NX - 1 and (n == 0 or half == 1))
                last.then_inc(S["o"], 1)
                pe.wait_ge(S["y"], n + 1)
                pe.wait_ge(S["St"], min(n + 1, NC - 1))
                for b in range(B):
                    for k in range(KC):
                        last = nc.tensor.transpose(bank_s[:, (b * KC + k) * P:(b * KC + k + 1) * P], y[:, b, k * P:(k + 1) * P], ident)
                last.then_inc(S["yt"], 1)
                pe.wait_ge(S["yT"], n + 1)
                for b in range(B):
                    for k in range(KC):
                        last = nc.tensor.matmul(bank_s[:, b * C:(b + 1) * C], yT[:, b, k], wout[:, k], start=k == 0, stop=k == KC - 1)
                last.then_inc(S["out"], 1)

        @blk.scalar
        def _(act):
            for n in range(NC):
                e = n % 2
                if n:
                    act.wait_ge(S["Xend"], n)
                for z in range(NX + 1):
                    act.wait_ge(S["z"], (NX + 2) * n + z + 1)
                    src = ps[:, z].rearrange("p (k b t) -> p k b t", k=KC, b=B)
                    if z == BASE:
                        nc.scalar.activation(F[:, 0], src, ACT.Exp, scale=-1.0)
                        nc.scalar.activation(F[:, NX], src, ACT.Exp).then_inc(S["F"], 1)
                    else:
                        nc.scalar.activation(F[:, z if z <= NL else NX + 1], src, ACT.Exp).then_inc(S["F"], 1)
                act.wait_ge(S["z"], (NX + 2) * (n + 1))
                nc.scalar.activation(Fend[:], bank_o.rearrange("p (b c) -> p b c", b=B), ACT.Exp).then_inc(S["F"], 1)
                act.wait_ge(S["o"], n + 1)
                nc.scalar.activation(y[:], bank_o.rearrange("p (b c) -> p b c", b=B), ACT.Copy).then_inc(S["y"], 1)
                act.wait_ge(S["yt"], n + 1)
                nc.scalar.activation(yT[:].rearrange("p b k t -> p (b k t)"), bank_s, ACT.Copy).then_inc(S["yT"], 1)

        @blk.vector
        def _(dve):
            nc.vector.memset(PM[:, NL], 0.0).then_inc(S["zero"], 1)
            nc.vector.memset(St[:], 0.0).then_inc(S["zero"], 1)
            dve.wait_ge(S["zero"], 2)
            for n in range(NC):
                e = n % 2
                dve.wait_ge(S["F"], (NX + 2) * (n + 1))
                src_k, src_r = kT_of(kT, n), kT_of(rT, n)
                if n:
                    dve.wait_ge(S["o"], n)
                nc.vector.tensor_tensor(Xend[:, e], Fend[:], kv[:].rearrange("p (b n) j c -> p b n j c", b=B)[:, :, n, 0],
                                        ALU.mult).then_inc(S["Xend"], 1)
                for k in range(KC):
                    nc.vector.tensor_tensor(XT[:, :, k], F[:, 0:NX, k], src_k[:, k].unsqueeze(1).broadcast_to([P, NX, B, P]), ALU.mult)
                for k in range(KC):
                    last = nc.vector.tensor_tensor(EF[:, :, k], F[:, 1:NX + 2, k],
                                                   src_r[:, k].unsqueeze(1).broadcast_to([P, NX + 1, B, P]), ALU.mult)
                last.then_inc(S["EF"], 1)
                if n < NC - 1:
                    dve.wait_ge(S["st"], n + 1)
                    if n:
                        dve.wait_ge(S["St"], n)
                    for half in range(2):
                        rows = slice(half * BD, (half + 1) * BD)
                        new = bank_s.rearrange("p (k b t) -> p k b t", k=KC, b=B)[rows, :, :, rows]
                        if n == 0:
                            last = nc.vector.tensor_copy(St[rows, 0, :, :, rows], new)
                        else:
                            for k in range(KC):
                                for b in range(B):
                                    last = nc.vector.scalar_tensor_tensor(
                                        St[rows, e, k, b, rows], St[rows, 1 - e, k, b, rows], F[rows, NX + 1, k, b, P - 1:P],
                                        new[:, k, b], ALU.mult, ALU.add)
                    last.then_inc(S["St"], 1)
                for u in range(UNITS):
                    xl, half = u // 2, u % 2
                    dve.wait_ge(S["P"], UNITS * n + u + 1)
                    src = ps[:, u % RING].rearrange("p (h t) -> p h t", t=P)
                    dst = PM[:, xl, half].rearrange("p k b t -> p (k b) t")
                    if xl < NL:
                        nc.vector.tensor_tensor(dst, src, mask[:, xl + 1].unsqueeze(1).broadcast_to([P, BH, P]),
                                                ALU.mult).then_inc(S["PM"], 1)
                    else:
                        nc.vector.copy_predicated(dst, mask[:, BASE].bitcast(U32).unsqueeze(1).broadcast_to([P, BH, P]),
                                                  src).then_inc(S["PM"], 1)
                dve.wait_ge(S["out"], n + 1)
                for b in range(B):
                    nc.vector.tensor_tensor(x[:, b * NC + n], x[:, b * NC + n], bank_s[:, b * C:(b + 1) * C], ALU.add)\
                        .then_inc(S["x"], 1)
            dve.wait_ge(S["x"], 2 * NC)


def mixer(nc, w, out):
    x_in = w["L0_attn_a_hidden_states"]
    with ExitStack() as ctx:
        def sb(name, shape, dt=F32):
            return ctx.enter_context(nc.sbuf_tensor(name, shape, dt))
        x = sb("x", [P, TILES, HID])
        hT = sb("hT", [P, KC, TILES * P])
        const = sb("const", [P, N_CONST])
        beta_rows = sb("beta_rows", [P, TILES, H])
        l_all = sb("l_all", [P, H, TILES])
        g_dram = nc.dram_tensor("g_scratch", [H, P, TILES, D], F32, kind="Internal").ap()
        o_dram = nc.dram_tensor("o_scratch", [TILES, P, H * D], F32, kind="Internal").ap()
        n_sum, n_mask = (NL + 3) * P, (NL + 1) * P
        consts = {"sums": const[:, 0:n_sum].rearrange("p (l t) -> p l t", t=P),
                  "mask": const[:, n_sum:n_sum + n_mask].rearrange("p (l t) -> p l t", t=P),
                  "ident": const[:, n_sum + n_mask:n_sum + n_mask + P],
                  "before": const[:, n_sum + n_mask + P:N_CONST]}
        ident = consts["ident"]

        with Phase(nc, "load") as ph:
            loaded = ph.sem("loaded")
            blk = ph.block()

            @blk.sync
            def _(sp):
                sp.dma_start(x[:], x_in.rearrange("b (n p) c -> p (b n) c", p=P)).then_inc(loaded, 16)
                sp.dma_start(const[:], w["constants"]).then_inc(loaded, 16)
                sp.wait_ge(loaded, 32)

        layer_norm(nc, "ln1", x, ident, hT)
        slot_decays(nc, hT, w, beta_rows, g_dram)
        slot_attention(nc, hT, w, consts, beta_rows, g_dram, o_dram, l_all)
        gated_output(nc, x, hT, w, ident, o_dram, l_all)
        W = {"gate": sb("w_gate", [P, KC, NE]), "shared_up": sb("w_shared_up", [P, KC, 2 * SH]),
             "shared_down": sb("w_shared_down", [SH, HID]), "up": sb("w_up", [P, KC, NE, 2 * EH]),
             "down": sb("w_down", [P, NE * EH // P, HID])}
        loads = [(W[n][:], w[f"L0_ffn_w_{n}"].rearrange("(k p) n -> p k n", p=P)) for n in ("gate", "shared_up")]
        loads += [(W["shared_down"][:], w["L0_ffn_w_shared_down"])]
        loads += [(W["up"][:, k], w["L0_ffn_w_up"].rearrange("e (k p) n -> k p e n", p=P)[k]) for k in range(KC)]
        loads += [(W["down"][:], w["L0_ffn_w_down"].rearrange("e h c -> (e h) c").rearrange("(q p) c -> p q c", p=P))]
        layer_norm(nc, "ln2", x, ident, hT, loads=loads)
        experts(nc, "ffn1", x, hT, W, consts)
        layer_norm(nc, "ln3", x, ident, hT, w["L0_attn_b_gamma"], w["L0_attn_b_beta"])
        linear_attention(nc, x, hT, w, consts)
        layer_norm(nc, "ln4", x, ident, hT)
        experts(nc, "ffn2", x, hT, W, consts)

        with Phase(nc, "store") as ph:
            stored = ph.sem("stored")
            blk = ph.block()

            @blk.sync
            def _(sp):
                sp.dma_start(out.rearrange("b (n p) c -> p (b n) c", p=P), x[:]).then_inc(stored, 16)
                sp.wait_ge(stored, 16)


_INS = ["L0_attn_a_hidden_states", *(f"L0_attn_a_{n}" for n in (
    "Wq Wk Wv Ww cq ck cv Wf1 Wf2 Wb Wg1 Wg2 bg2 norm_w Wo").split()),
    *(f"L0_attn_b_{n}" for n in "Wx Ww bw Wk Wv Wr Wout gamma beta".split()),
    *(f"L0_ffn_{n}" for n in "w_gate w_shared_up w_shared_down w_up w_down".split())]


def kernel(**inputs):
    import numpy as _np
    import concourse.bacc as _bacc
    from concourse import mybir as _mybir
    from concourse.bass_utils import run_bass_kernel_spmd as _run

    nc = _bacc.Bacc("TRN2", target_bir_lowering=False, num_devices=1)
    arrays, w = {}, {}
    for name in _INS + ["constants"]:
        a = constants() if name == "constants" else _np.ascontiguousarray(inputs[name])
        arrays[f"in_{name}"] = a
        w[name] = nc.dram_tensor(f"in_{name}", a.shape, _mybir.dt.from_np(a.dtype), kind="ExternalInput").ap()
    out = nc.dram_tensor("out_0", (B, T, HID), F32, kind="ExternalOutput").ap()
    mixer(nc, w, out)
    r = _run(nc, [arrays], core_ids=[0])
    return r.results[0]["out_0"]
```

```python
from contextlib import ExitStack

import numpy as np

import concourse.bass as bass
from concourse import mybir
from concourse.alu_op_type import AluOpType as ALU

F32 = mybir.dt.float32
U32 = mybir.dt.uint32
I32 = mybir.dt.int32
ACT = mybir.ActivationFunctionType
X = mybir.AxisListType.X
P = 128

B, T, HID = 2, 512, 256
TILES = B * T // P
NC = T // P
KC = HID // P
H, D = 16, 128
KW = 4
SCALE = float(D) ** -0.5
EPS = 1e-5
BH, BD = 4, 64
NE, EH, TOPK, CAP = 64, 32, 6, 128
SH = 64
FLOOR = 20.0
SUB = 8
LEVELS = (8, 16, 32, 64)
NL = len(LEVELS)
BASE, START, END = 0, NL + 1, NL + 2


def constants():
    j, t = np.arange(P)[:, None], np.arange(P)[None, :]
    sums = np.zeros((P, NL + 3, P), np.float32)
    mask = np.zeros((P, NL + 1, P), np.float32)
    mid = t - t % SUB + SUB // 2
    sums[:, BASE] = 1.0 * ((j >= mid) & (j <= t)) - 1.0 * ((j > t) & (j < mid)) - 0.5 * (j == mid)
    mask[:, BASE] = (j // SUB == t // SUB) & (j <= t)
    half = np.zeros((P, NL, B, P // 2), np.float32)
    for n, size in enumerate(LEVELS):
        mid = t - t % (2 * size) + size
        sums[:, n + 1] = ((j >= mid) & (j <= t)) | ((j > t) & (j < mid))
        mask[:, n + 1] = (j // (2 * size) == t // (2 * size)) & (j % (2 * size) < size) & (t % (2 * size) >= size)
        half[:, n] = mask[:, n + 1].reshape(P, -1, 2, size)[:, :, 1].reshape(P, 1, P // 2)
    sums[:, START] = j <= t
    sums[:, END] = j > t
    before = (j < t).astype(np.float32)
    base = np.repeat(mask[:, BASE][:, None], B, axis=1)
    return np.concatenate([a.reshape(P, -1) for a in (sums, mask, np.eye(P, dtype=np.float32), before, half, base)], axis=1)


CONST_AT = np.cumsum([0, (NL + 3) * P, (NL + 1) * P, P, P, NL * B * P // 2, B * P]).tolist()
N_CONST = CONST_AT[-1]


def left(ap, size):
    return ap.rearrange("p b (k two s) -> p b k two s", two=2, s=size)[:, :, :, 0]


def right(ap, size):
    return ap.rearrange("p b (k two s) -> p (b k) two s", two=2, s=size)[:, :, 1]


def together(ap, size):
    return ap.rearrange("p b (k s) -> p (b k) s", s=size)


class Phase:

    def __init__(self, nc, name):
        self.nc, self.name, self.ctx, self.sems = nc, name, ExitStack(), []

    def __enter__(self):
        self.ctx.__enter__()
        return self

    def __exit__(self, *a):
        left = self.ctx.__exit__(*a)
        if self.sems:
            self.nc.clear_and_free_semaphores(self.sems)
        return left

    def sb(self, name, shape, dt=F32):
        return self.ctx.enter_context(self.nc.sbuf_tensor(f"{self.name}_{name}", shape, dt))

    def ps(self, name, shape, dt=F32):
        return self.ctx.enter_context(self.nc.psum_tensor(f"{self.name}_{name}", shape, dt))

    def sem(self, name):
        self.sems.append(self.nc.alloc_semaphore(f"{self.name}_{name}", num=self.nc.free_semaphores[-1]))
        return self.sems[-1]

    def block(self):
        return self.ctx.enter_context(self.nc.Block())


def after(eng, sem, count):
    if not isinstance(count, int) or count > 0:
        eng.wait_ge(sem, count)


def by_tiles(eng, tile):
    for t in range(2):
        tile(t, t)
    with eng.Fori(1, TILES // 2) as i:
        for par in range(2):
            tile(2 * i + par, par)


def by_tiles_ahead(eng, step):
    for t in range(2):
        step(t, t, True)
    with eng.Fori(1, TILES // 2 - 1) as i:
        for par in range(2):
            step(2 * i + par, par, True)
    for par in range(2):
        step(TILES - 2 + par, par, par == 0)


def layer_norm(nc, name, x, ident, hT, gamma=None, beta=None, loads=()):
    with Phase(nc, name) as ph:
        stats = ph.sb("stats", [P, TILES, 6])
        mv = ph.sb("mv", [P, TILES, 2])
        std = ph.sb("std", [P, TILES])
        rstd = ph.sb("rstd", [P, TILES])
        shift = ph.sb("shift", [P, TILES])
        h = ph.sb("h", [P, TILES, HID])
        eps = ph.sb("eps", [P, 1])
        turned = ph.ps("turned", [P, 4, 512])
        loaded, eps_set, gb_in = ph.sem("loaded"), ph.sem("eps_set"), ph.sem("gb_in")
        stats_done, mv_done, std_done, rstd_done = (ph.sem(s) for s in ("stats_done", "mv_done", "std_done", "rstd_done"))
        shift_done, h_ready, turned_ready, copied = (ph.sem(s) for s in ("shift_done", "h_ready", "turned_ready", "copied"))
        gb = ph.sb("gb", [P, 2, KC])
        blk = ph.block()

        @blk.sync
        def _(sp):
            for dst, src in loads:
                sp.dma_start(dst, src).then_inc(loaded, 16)
            if gamma is not None:
                sp.dma_start(gb[:, 0, :], gamma.rearrange("(k p) -> p k", p=P), allow_slow_non_contiguous=True).then_inc(gb_in, 16)
                sp.dma_start(gb[:, 1, :], beta.rearrange("(k p) -> p k", p=P), allow_slow_non_contiguous=True).then_inc(gb_in, 16)
            if loads:
                sp.wait_ge(loaded, 16 * len(loads))

        @blk.vector
        def _(dve):
            nc.vector.memset(eps[:], EPS).then_inc(eps_set, 1)
            for n in range(TILES):
                nc.vector.bn_stats(stats[:, n, :], x[:, n, :]).then_inc(stats_done, 1)
            for n in range(TILES):
                dve.wait_ge(stats_done, n + 1)
                nc.vector.bn_aggr(mv[:, n, :], stats[:, n, :]).then_inc(mv_done, 1)
            dve.wait_ge(std_done, 1)
            nc.vector.reciprocal(rstd[:], std[:]).then_inc(rstd_done, 1)
            dve.wait_ge(rstd_done, 1)
            nc.vector.scalar_tensor_tensor(shift[:], mv[:, :, 0], -1.0, rstd[:], ALU.mult, ALU.mult).then_inc(shift_done, 1)
            dve.wait_ge(shift_done, 1)
            for n in range(TILES):
                nc.vector.tensor_scalar(h[:, n, :], x[:, n, :], rstd[:, n:n + 1], shift[:, n:n + 1],
                                        ALU.mult, ALU.add).then_inc(h_ready, 1)

        @blk.tensor
        def _(pe):
            for n in range(TILES):
                pe.wait_ge(h_ready, n + 1)
                for k in range(KC):
                    last = nc.tensor.transpose(turned[:, n // 2, (n % 2 + 2 * k) * P:(n % 2 + 2 * k + 1) * P],
                                               h[:, n, k * P:(k + 1) * P], ident)
                last.then_inc(turned_ready, 1)

        @blk.scalar
        def _(act):
            act.wait_ge(mv_done, TILES)
            act.wait_ge(eps_set, 1)
            nc.scalar.activation(std[:], mv[:, :, 1], ACT.Sqrt, bias=eps[:, 0:1]).then_inc(std_done, 1)
            if gamma is not None:
                act.wait_ge(gb_in, 32)
            for pair in range(TILES // 2):
                act.wait_ge(turned_ready, 2 * pair + 2)
                for k in range(KC):
                    dst = hT[:, k, 2 * pair * P:(2 * pair + 2) * P]
                    src = turned[:, pair, 2 * k * P:(2 * k + 2) * P]
                    if gamma is None:
                        nc.scalar.activation(dst, src, ACT.Copy).then_inc(copied, 1)
                    else:
                        nc.scalar.activation(dst, src, ACT.Identity, bias=gb[:, 1, k:k + 1],
                                             scale=gb[:, 0, k:k + 1]).then_inc(copied, 1)
            act.wait_ge(copied, TILES // 2 * KC)


def slot_decays(nc, hT, w, beta_rows, g_dram):
    HF = H * D // 2
    with Phase(nc, "decay") as ph:
        wf1, wb = ph.sb("wf1", [P, KC, D]), ph.sb("wb", [P, KC, H])
        wf2 = ph.sb("wf2", [P, H * D])
        fT = ph.sb("fT", [P, TILES * P])
        away = ph.sb("away", [P, 2, HF])
        e = ph.sb("e", [P, 2 * TILES, HF])
        low = ph.sb("low", [P, 2 * TILES, HF])
        ln = ph.sb("ln", [P, 2, HF])
        g = ph.sb("g", [P, 2, HF])
        tb = ph.sb("tb", [P, TILES, H])
        psf = ph.ps("psf", [P, 2, 512])
        psg = ph.ps("psg", [P, 2, HF])
        psb = ph.ps("psb", [P, TILES, H])
        loaded = ph.sem("loaded")
        f_ready, f_copied, b_ready, b_tanh, b_done = (ph.sem(s) for s in ("f_ready", "f_copied", "b_ready", "b_tanh", "b_done"))
        g_raw, g_abs, g_exp, g_low, g_ln, g_ready = (ph.sem(s) for s in "g_raw g_abs g_exp g_low g_ln g_ready".split())
        g_stored = [ph.sem(f"g_stored{n}") for n in range(2)]
        blk = ph.block()
        halves = 2 * TILES

        @blk.sync
        def _(sp):
            sp.dma_start(wf1[:], w["L0_attn_a_Wf1"].rearrange("(k p) n -> p k n", p=P)).then_inc(loaded, 16)
            sp.dma_start(wb[:], w["L0_attn_a_Wb"].rearrange("(k p) n -> p k n", p=P)).then_inc(loaded, 16)
            sp.dma_start(wf2[:], w["L0_attn_a_Wf2"]).then_inc(loaded, 16)
            for q in range(halves):
                sp.wait_ge(g_ready, q + 1)
                sp.dma_start(g_dram[q % 2 * (H // 2):(q % 2 + 1) * (H // 2), :, q // 2, :].rearrange("h p m -> p h m"),
                             g[:, q % 2, :].rearrange("p (h m) -> p h m", m=D)).then_inc(g_stored[q % 2], 16)
            for n in range(2):
                sp.wait_ge(g_stored[n], 16 * TILES)

        @blk.tensor
        def _(pe):
            pe.wait_ge(loaded, 48)
            for half in range(2):
                for k in range(KC):
                    last = nc.tensor.matmul(psf[:, half, :], wf1[:, k, :], hT[:, k, half * 512:(half + 1) * 512],
                                            start=k == 0, stop=k == KC - 1)
                last.then_inc(f_ready, 1)
            for n in range(TILES):
                for k in range(KC):
                    last = nc.tensor.matmul(psb[:, n, :], hT[:, k, n * P:(n + 1) * P], wb[:, k, :],
                                            start=k == 0, stop=k == KC - 1)
            last.then_inc(b_ready, 1)
            pe.wait_ge(f_copied, 2)
            for q in range(halves):
                if q >= 2:
                    pe.wait_ge(g_low, q - 1)
                for c in range(HF // 512):
                    last = nc.tensor.matmul(psg[:, q % 2, c * 512:(c + 1) * 512], fT[:, q // 2 * P:(q // 2 + 1) * P],
                                            wf2[:, q % 2 * HF + c * 512:q % 2 * HF + (c + 1) * 512], start=True, stop=True)
                last.then_inc(g_raw, 1)

        @blk.scalar
        def _(act):
            for q in range(halves):
                act.wait_ge(g_raw, q + 1)
                if q >= 2:
                    act.wait_ge(g_exp, q - 1)
                nc.scalar.activation(away[:, q % 2, :], psg[:, q % 2, :], ACT.Abs).then_inc(g_abs, 1)
                act.wait_ge(g_abs, q + 1)
                nc.scalar.activation(e[:, q, :], away[:, q % 2, :], ACT.Exp, scale=-1.0).then_inc(g_exp, 1)
            for q in range(halves):
                act.wait_ge(g_exp, q + 1)
                if q >= 2:
                    act.wait_ge(g_ready, q - 1)
                nc.scalar.activation(ln[:, q % 2, :], e[:, q, :], ACT.Ln, bias=1.0).then_inc(g_ln, 1)
            act.wait_ge(b_ready, 1)
            nc.scalar.activation(tb[:], psb[:], ACT.Tanh, scale=0.5).then_inc(b_tanh, 1)

        @blk.vector
        def _(dve):
            for half in range(2):
                dve.wait_ge(f_ready, half + 1)
                nc.vector.tensor_copy(fT[:, half * 512:(half + 1) * 512], psf[:, half, :]).then_inc(f_copied, 1)
            for q in range(halves):
                dve.wait_ge(g_abs, q + 1)
                nc.vector.tensor_scalar(low[:, q, :], psg[:, q % 2, :], 0.0, None, ALU.min).then_inc(g_low, 1)
            for q in range(halves):
                dve.wait_ge(g_low, q + 1)
                dve.wait_ge(g_ln, q + 1)
                if q >= 2:
                    dve.wait_ge(g_stored[q % 2], 16 * (q // 2))
                nc.vector.tensor_tensor(g[:, q % 2, :], low[:, q, :], ln[:, q % 2, :], ALU.subtract).then_inc(g_ready, 1)
            dve.wait_ge(b_tanh, 1)
            nc.vector.tensor_scalar(beta_rows[:], tb[:], 0.5, 0.5, ALU.mult, ALU.add).then_inc(b_done, 1)
            dve.wait_ge(b_done, 1)


def slot_attention(nc, hT, w, consts, beta_rows, g_dram, o_dram, l_all):
    sums, ident, half_mask, base_mask = consts["sums"], consts["ident"], consts["half"], consts["base"]
    NX = NL + 1
    HALF = P // 2
    names = ("q", "k", "v", "w")
    order = ("w", "k", "v", "q")
    NP = len(order)
    BM, BP, ST = 0, NX, NX + 1

    with Phase(nc, "gsa") as ph:
        weights = ph.sb("weights", [P, 2, 4, KC, D])
        taps_all = ph.sb("taps_all", [P, H, 3, KW])
        taps = ph.sb("taps", [P, 2, 3, KW])
        headT = {n: ph.sb(f"{n}T", [P, 2, B, T]) for n in names}
        pieceT = ph.sb("pieceT", [P, B, T])
        raw = ph.sb("raw", [P, B, T])
        tanh = ph.sb("tanh", [P, B, T])
        wsq = ph.sb("wsq", [P, B, T])
        ones = ph.sb("ones", [P, 1])
        ss = ph.sb("ss", [P, 3, TILES])
        half3 = ph.sb("half3", [P, 1])
        nwt = ph.sb("nwt", [P, 5, TILES])
        c = ph.sb("c", [P, 2, B, NC])
        g = ph.sb("g", [P, 2, B, NC, D])
        gf = ph.sb("gf", [P, 2, B, NC, D])
        FT = ph.sb("FT", [P, 2, NX + 2, B, P])
        Fend = ph.sb("Fend", [P, B, D])
        wR = ph.sb("wR", [P, B, D])
        kv = ph.sb("kv", [P, 2, B, 2 * D])
        XT = ph.sb("XT", [P, 2, NX, B, P])
        XR = ph.sb("XR", [P, B, NX, D])
        Xend = ph.sb("Xend", [P, 2, B, D])
        AL = ph.sb("AL", [P, NL, B, HALF])
        AB = ph.sb("AB", [P, B, P])
        PT = ph.sb("PT", [P, NX + 1, B, P])
        negmax = ph.sb("negmax", [P, B])
        bias = ph.sb("bias", [P, B])
        a = ph.sb("a", [P, B, D])
        l = ph.sb("l", [P, 2, B, NC])
        aL = ph.sb("aL", [P, NL, B, HALF])
        aB = ph.sb("aB", [P, 2, B, P])
        seen = ph.sb("seen", [P, 1])
        PM = ph.sb("PM", [P, B, P])
        KV = ph.sb("KV", [P, 2, B, 2 * D])
        Sk = ph.sb("Sk", [P, B, D])
        o = ph.sb("o", [P, 2, B, NC, D])
        UL = ph.ps("UL", [P, NL, B, HALF])
        UB = ph.ps("UB", [P, 2, B, P])
        UR = ph.ps("UR", [P, 2, B, P])
        V = ph.ps("V", [P, 3, 512])
        B6 = ph.ps("B6", [P, 2, B, D])
        B7 = ph.ps("B7", [P, 2, B, D])
        Vproj = V[:, 0:2].rearrange("p x n -> p (x n)")

        S = {n: ph.sem(n) for n in (
            "taps_in taps_halved taps_set g_floored ones_set zeros_set half3_set o_out "
            "pe_wk pe_vA pe_z pe_S pe_rows pe_aT pe_St pe_XR pe_P pe_SkT pe_O pe_proj pe_ss "
            "act_w act_kv act_z act_a act_XB act_XR act_Sk act_O act_piece act_tap act_tanh act_sq "
            "dve_A dve_prod dve_max dve_bias dve_aF dve_PM dve_KV dve_conv dve_silu dve_ss dve_g1 "
            "pool_c pool_n pool_l pool_XT pool_end").split()}
        w_in = [ph.sem(f"w_in{n}") for n in range(2)]
        g_in = [ph.sem(f"g_in{n}") for n in range(2)]
        blk = ph.block()


        def pe_project(pe, h, hp, p, es=None):
            q = NP * h + p
            if p == 0:
                pe.wait_ge(w_in[hp], 32 * (h - hp) + 64)
            after(pe, S["act_piece"], q)
            for x in range(B):
                if es is not None:
                    pe.wait_ge(S[("act_XB", "act_XR")[x]], es + 1)
                for k in range(KC):
                    last = nc.tensor.matmul(Vproj[:, x * T:(x + 1) * T], weights[:, hp, names.index(order[p]), k, :],
                                            hT[:, k, x * T:(x + 1) * T], start=k == 0, stop=k == KC - 1)
            last.then_inc(S["pe_proj"], 1)

        def pe_sumsq(pe, h):
            pe.wait_ge(S["act_sq"], h + 1)
            for t in range(TILES):
                last = nc.tensor.matmul(UR[:, 1, 0, t:t + 1], wsq[:, t // NC, t % NC * P:(t % NC + 1) * P],
                                        ones[:], start=True, stop=True)
            last.then_inc(S["pe_ss"], 1)

        def pe_early(pe, eh, en, ep, es, st, prologue):
            tile = slice(en * P, (en + 1) * P)
            pe.wait_ge(S["dve_silu"], NP * (eh + 1))
            if not prologue:
                after(pe, S["act_O"], es - 1)
            for j, name in enumerate(("w", "k")):
                for b in range(B):
                    last = nc.tensor.transpose(B6[:, j, b, :], headT[name][:, ep, b, tile], ident)
            last.then_inc(S["pe_wk"], 1)
            if not prologue:
                after(pe, S["act_Sk"], st)
            for b in range(B):
                nc.tensor.transpose(B7[:, 0, b, :], headT["v"][:, ep, b, tile], ident)
            for b in range(B):
                last = nc.tensor.matmul(B7[:, 1, b, :], headT["k"][:, ep, b, tile], headT["q"][:, ep, b, tile],
                                        start=True, stop=True)
            last.then_inc(S["pe_vA"], 1)

        def pe_sums(pe, eh, en, ep, es, zs, pieces):
            if 0 in zs:
                pe.wait_ge(S["g_floored"], eh + 1)
                pe.wait_ge(S["act_piece"], pieces)
            for z in zs:
                if z == 3:
                    pe.wait_ge(S["act_z"], 4 * es + 1)
                    last = nc.tensor.matmul(V[:, 0, 0:B * D], sums[:, END, :], g[:, ep, :, en, :], start=True, stop=True)
                else:
                    for x in range(2):
                        place = 2 * z + x
                        gz = gf if place == BASE else g
                        for b in range(B):
                            last = nc.tensor.matmul(V[:, z, (x * B + b) * P:(x * B + b + 1) * P], gz[:, ep, b, en, :],
                                                    sums[:, place, :], start=True, stop=True)
                last.then_inc(S["pe_z"], 1)

        def pe_XR(pe, en, es):
            pe.wait_ge(S["act_z"], 4 * es + 4)
            pe.wait_ge(S["pool_XT"], es + 1)
            for b in range(B):
                nc.tensor.transpose(V[:, 0, (2 + b) * P:(3 + b) * P], XT[:, en % 2, BM, b, :], ident)
            for b in range(B):
                for x in range(NL):
                    last = nc.tensor.transpose(V[:, 1 + b, x * P:(x + 1) * P], XT[:, en % 2, 1 + x, b, :], ident)
            last.then_inc(S["pe_XR"], 1)

        def pe_step(pe, h, n, hp, early, ready, piece, last_head):
            s, st = NC * h + n, (NC - 1) * h + n
            e = n % 2
            pe.wait_ge(S["act_XR"], s + 1)
            pe.wait_ge(S["dve_A"], s + 1)
            after(pe, S["dve_PM"], NX * s)
            for x in range(NL):
                for b in range(B):
                    last = nc.tensor.matmul(UL[:, x, b, :], XR[:, b, 1 + x, :], AL[:, x, b, :], start=True, stop=True)
            for b in range(B):
                last = nc.tensor.matmul(UB[:, 0, b, :], XR[:, b, BM, :], AB[:, b, :], start=True, stop=True)
            if n > 0:
                pe.wait_ge(S["act_Sk"], st)
                for b in range(B):
                    last = nc.tensor.matmul(UB[:, 1, b, :], Sk[:, b, :], headT["q"][:, hp, b, n * P:(n + 1) * P],
                                            start=True, stop=True)
            last.then_inc(S["pe_S"], 1)
            if early:
                pe_early(pe, *early, False)
                pieces = NP * (h + 1) + n + 2
                if isinstance(h, int):
                    pieces = min(pieces, NP * H)
                pe_sums(pe, *early[:4], (0,), pieces)
            pe.wait_ge(S["dve_prod"], s + 1)
            after(pe, S["act_a"], s)
            if n == 1 and not last_head:
                after(pe, S["dve_ss"], h + 2)
            parts = NX + (n > 0)
            for b in range(B):
                for x in range(parts):
                    last = nc.tensor.matmul(UR[:, 0, b, :], PT[:, x, b, :], ident, is_transpose=True,
                                            start=x == 0, stop=x == parts - 1)
            last.then_inc(S["pe_rows"], 1)
            if early:
                pe_sums(pe, *early[:4], (1, 2), pieces)
            pe.wait_ge(S["act_a"], s + 1)
            if early:
                pe.wait_ge(S["act_kv"], s + 2)
            for b in range(B):
                last = nc.tensor.transpose(B6[:, 0, b, :], a[:, b, :], ident)
            last.then_inc(S["pe_aT"], 1)
            if n < NC - 1:
                pe.wait_ge(S["pool_end"], s + 1)
                pe.wait_ge(S["dve_A"], s + 2)
                for b in range(B):
                    last = nc.tensor.matmul(B7[:, b, :, :], Xend[:, e, b, :], kv[:, e, b, :], start=True, stop=True)
                last.then_inc(S["pe_St"], 1)
            if early:
                pe_sums(pe, *early[:4], (3,), pieces)
            if n == 0 and not last_head:
                pe_sumsq(pe, h + 1)
            pe.wait_ge(S["dve_aF"], s + 1)
            for x in range(NL):
                for b in range(B):
                    nc.tensor.matmul(UL[:, x, b, :], XT[:, e, 1 + x, b, :], aL[:, x, b, :], start=True, stop=True)
            for b in range(B):
                last = nc.tensor.matmul(UB[:, 0, b, :], XT[:, e, BM, b, :], aB[:, 0, b, :], start=True, stop=True)
            last.then_inc(S["pe_P"], 1)
            if early:
                pe_XR(pe, early[1], early[3])
            if n < NC - 1:
                pe.wait_ge(S["dve_KV"], st + 1)
                for b in range(B):
                    last = nc.tensor.transpose(B7[:, 0, b, :], KV[:, n % 2, b, 0:D], ident)
                last.then_inc(S["pe_SkT"], 1)
            if piece:
                pe_project(pe, *piece, s + 1)
            pe.wait_ge(S["dve_PM"], NX * (s + 1))
            for b in range(B):
                last = nc.tensor.matmul(B6[:, 0, b, :], PM[:, b, :], kv[:, e, b, D:2 * D], start=True, stop=n == 0)
                if n > 0:
                    last = nc.tensor.matmul(B6[:, 0, b, :], aB[:, 1, b, :], KV[:, (n - 1) % 2, b, D:2 * D],
                                            start=False, stop=True)
            last.then_inc(S["pe_O"], 1)

        def act_piece(act, h, hp, p):
            q = NP * h + p
            if p == 0:
                act.wait_ge(S["taps_set"], h + 1)
            act.wait_ge(S["pe_proj"], q + 1)
            after(act, S["dve_silu"], q)
            nc.scalar.activation(pieceT[:].rearrange("p b t -> p (b t)"), Vproj, ACT.Copy).then_inc(S["act_piece"], 1)
            act.wait_ge(S["act_piece"], q + 1)
            j = min(names.index(order[p]), 2)
            nc.scalar.activation(raw[:], pieceT[:], ACT.Copy, scale=taps[:, hp, j, KW - 1:KW]).then_inc(S["act_tap"], 1)

        def act_tanh(act, h, hp, p):
            act.wait_ge(S["dve_conv"], (KW - 1) * (NP * h + p + 1))
            nc.scalar.activation(tanh[:], raw[:], ACT.Tanh).then_inc(S["act_tanh"], 1)

        def act_sq(act, h, hp, p):
            if p == 0:
                act.wait_ge(S["dve_silu"], NP * h + 1)
                after(act, S["pe_ss"], h)
                nc.scalar.activation(wsq[:], headT["w"][:, hp], ACT.Square).then_inc(S["act_sq"], 1)

        def act_rows(act, eh, en, ep, es, st, prologue):
            ee = en % 2
            act.wait_ge(S["pe_wk"], es + 1)
            if not prologue:
                after(act, S["pool_end"], es)
            nc.scalar.activation(wR[:], B6[:, 0], ACT.Copy).then_inc(S["act_w"], 1)
            act.wait_ge(S["pool_c"], eh + 1)
            if not prologue:
                after(act, S["pe_O"], es - 1)
            for b in range(B):
                nc.scalar.activation(kv[:, ee, b, 0:D], B6[:, 1, b, :], ACT.Copy, scale=c[:, ep, b, en:en + 1])
            act.wait_ge(S["pe_vA"], es + 1)
            for b in range(B):
                last = nc.scalar.activation(kv[:, ee, b, D:2 * D], B7[:, 0, b, :], ACT.Copy, scale=c[:, ep, b, en:en + 1])
            last.then_inc(S["act_kv"], 1)

        def act_factors(act, en, es, zs):
            ee = en % 2
            F = [V[:, z].rearrange("p (x b t) -> p x b t", x=2, b=B) for z in range(3)]
            for z in zs:
                act.wait_ge(S["pe_z"], 4 * es + z + 1)
                if z == 0:
                    nc.scalar.activation(FT[:, ee, BM], F[0][:, 0], ACT.Exp, scale=-1.0)
                    nc.scalar.activation(FT[:, ee, BP], F[0][:, 0], ACT.Exp)
                    last = nc.scalar.activation(FT[:, ee, 1], F[0][:, 1], ACT.Exp)
                elif z == 1:
                    last = nc.scalar.activation(FT[:, ee, 2:4], F[1], ACT.Exp)
                else:
                    nc.scalar.activation(FT[:, ee, 4], F[2][:, 0], ACT.Exp)
                    last = nc.scalar.activation(FT[:, ee, ST], F[2][:, 1], ACT.Exp)
                last.then_inc(S["act_z"], 1)

        def act_end(act, es, prologue):
            act.wait_ge(S["pe_z"], 4 * es + 4)
            if not prologue:
                after(act, S["pool_end"], es)
            nc.scalar.activation(Fend[:].rearrange("p b d -> p (b d)"), V[:, 0, 0:B * D], ACT.Exp).then_inc(S["act_z"], 1)

        def act_XR(act, en, ep, es, prologue):
            act.wait_ge(S["pe_XR"], es + 1)
            if not prologue:
                after(act, S["pe_S"], es)
            for b in range(B):
                last = nc.scalar.activation(XR[:, b, BM, :], V[:, 0, (2 + b) * P:(3 + b) * P], ACT.Copy,
                                            scale=c[:, ep, b, en:en + 1])
            last.then_inc(S["act_XB"], 1)
            for b in range(B):
                last = nc.scalar.activation(XR[:, b, 1:NX, :].rearrange("p x d -> p (x d)"), V[:, 1 + b], ACT.Copy,
                                            scale=c[:, ep, b, en:en + 1])
            last.then_inc(S["act_XR"], 1)

        def act_step(act, h, n, hp, early, ready, piece, last_head):
            s, st = NC * h + n, (NC - 1) * h + n
            if early:
                act_rows(act, *early, False)
                act_factors(act, early[1], early[3], (0,))
            act.wait_ge(S["dve_bias"], s + 1)
            after(act, S["pe_aT"], s)
            if n == 0:
                after(act, S["pool_l"], h - 1)
            for b in range(B):
                last = nc.scalar.activation(a[:, b, :], UR[:, 0, b, :], ACT.Exp, bias=bias[:, b:b + 1], scale=SCALE,
                                            accum_out=l[:, hp, b, n:n + 1])
            last.then_inc(S["act_a"], 1)
            if early:
                act_factors(act, early[1], early[3], (1, 2))
                act_end(act, early[3], False)
            if ready:
                act_tanh(act, *ready)
            if early:
                act_XR(act, early[1], early[2], early[3], False)
            if n < NC - 1:
                act.wait_ge(S["pe_SkT"], st + 1)
                nc.scalar.activation(Sk[:], B7[:, 0], ACT.Copy).then_inc(S["act_Sk"], 1)
            if ready:
                act_sq(act, *ready)
            if piece:
                act_piece(act, *piece)
            act.wait_ge(S["pe_O"], s + 1)
            if n == 0:
                after(act, S["o_out"], 16 * h)
            nc.scalar.activation(o[:, hp, :, n, :], B6[:, 0], ACT.Copy).then_inc(S["act_O"], 1)

        def dve_conv(dve, h, hp, p, backs):
            q = NP * h + p
            j = min(names.index(order[p]), 2)
            for back in backs:
                if back == 1:
                    dve.wait_ge(S["act_tap"], q + 1)
                else:
                    dve.wait_ge(S["dve_conv"], (KW - 1) * q + back - 1)
                nc.vector.scalar_tensor_tensor(raw[:, :, back:T], pieceT[:, :, 0:T - back],
                                               taps[:, hp, j, KW - 1 - back:KW - back], raw[:, :, back:T],
                                               ALU.mult, ALU.add).then_inc(S["dve_conv"], 1)

        def dve_silu(dve, h, hp, p):
            dve.wait_ge(S["act_tanh"], NP * h + p + 1)
            nc.vector.scalar_tensor_tensor(headT[order[p]][:, hp], tanh[:], 1.0, raw[:], ALU.add, ALU.mult)\
                .then_inc(S["dve_silu"], 1)

        def dve_sumsq(dve, h):
            dve.wait_ge(S["pe_ss"], h + 1)
            after(dve, S["pool_c"], h)
            nc.vector.tensor_scalar(ss[:, 0], UR[:, 1, 0, 0:TILES], 1e-6, None, ALU.add).then_inc(S["dve_g1"], 1)
            dve.wait_ge(S["dve_g1"], 3 * h + 1)
            nc.vector.tensor_scalar(ss[:, 1].bitcast(I32), ss[:, 0].bitcast(I32), 1, None,
                                    ALU.logical_shift_right).then_inc(S["dve_g1"], 1)
            nc.vector.tensor_scalar(ss[:, 2], ss[:, 0], -0.5, None, ALU.mult).then_inc(S["dve_g1"], 1)
            dve.wait_ge(S["dve_g1"], 3 * h + 3)
            nc.vector.tensor_scalar(nwt[:, 0].bitcast(I32), ss[:, 1].bitcast(I32), -1.0, float(0x5f3759df),
                                    ALU.mult, ALU.add).then_inc(S["dve_ss"], 1)

        def dve_A(dve, es):
            dve.wait_ge(S["act_kv"], es + 1)
            for x, size in enumerate(LEVELS):
                nc.vector.tensor_tensor(together(AL[:, x], size), right(B7[:, 1], size), together(half_mask[:, x], size), ALU.mult)
            nc.vector.tensor_tensor(AB[:], B7[:, 1], base_mask, ALU.mult).then_inc(S["dve_A"], 1)

        def dve_floor(dve, h, hp):
            dve.wait_ge(g_in[hp], 8 * (h - hp) + 16)
            nc.vector.tensor_scalar(gf[:, hp], g[:, hp], -FLOOR, None, ALU.max).then_inc(S["g_floored"], 1)

        def dve_step(dve, h, n, hp, early, ready, piece, last_head):
            s, st = NC * h + n, (NC - 1) * h + n
            e = n % 2
            dve.wait_ge(S["pe_S"], s + 1)
            after(dve, S["pe_rows"], s)
            for x, size in enumerate(LEVELS):
                last = nc.vector.tensor_tensor(right(PT[:, x], size), together(UL[:, x], size), right(FT[:, e, 1 + x], size), ALU.mult)
            k = 1 + (n > 0)
            nc.vector.tensor_tensor(PT[:, NL:NL + k], UB[:, 0:k], FT[:, e, BP:BP + k], ALU.mult).then_inc(S["dve_prod"], 1)
            if ready:
                dve_conv(dve, *ready, (1,))
            dve.wait_ge(S["pe_rows"], s + 1)
            nc.vector.tensor_reduce(negmax[:], UR[:, 0], X, ALU.max, negate=True).then_inc(S["dve_max"], 1)
            dve.wait_ge(S["dve_max"], s + 1)
            nc.vector.tensor_scalar(bias[:], negmax[:], SCALE, None, ALU.mult).then_inc(S["dve_bias"], 1)
            if early:
                dve_A(dve, early[3])
            dve.wait_ge(S["pe_aT"], s + 1)
            after(dve, S["pe_O"], s)
            for x, size in enumerate(LEVELS):
                nc.vector.tensor_tensor(together(aL[:, x], size), right(FT[:, e, 1 + x], size), right(B6[:, 0], size), ALU.mult)
            nc.vector.tensor_tensor(aB[:, 0:k], FT[:, e, BP:BP + k], B6[:, 0].unsqueeze(1).broadcast_to([P, k, B, P]),
                                    ALU.mult).then_inc(S["dve_aF"], 1)
            if ready:
                dve_conv(dve, *ready, (2, 3))
            if n < NC - 1:
                dve.wait_ge(S["pe_St"], st + 1)
                if n == 0:
                    nc.vector.tensor_copy(KV[:, 0], B7[:].rearrange("p x b d -> p x (b d)")).then_inc(S["dve_KV"], 1)
                else:
                    dve.wait_ge(S["dve_KV"], st)
                    for b in range(B):
                        last = nc.vector.scalar_tensor_tensor(KV[:, n % 2, b], KV[:, (n - 1) % 2, b],
                                                              FT[:, e, ST, b, P - 1:P],
                                                              B7[:, b].rearrange("p b d -> p (b d)"), ALU.mult, ALU.add)
                    last.then_inc(S["dve_KV"], 1)
            if n == 0 and not last_head:
                dve_sumsq(dve, h + 1)
            if n == 2 and not last_head:
                dve_floor(dve, h + 1, 1 - hp)
            if ready:
                dve_silu(dve, *ready)
            dve.wait_ge(S["pe_P"], s + 1)
            for x, size in enumerate(LEVELS):
                if x == 0:
                    nc.vector.tensor_tensor(right(PM[:], size), together(UL[:, x], size), together(half_mask[:, x], size),
                                            ALU.mult).then_inc(S["dve_PM"], 1)
                else:
                    dve.wait_ge(S["dve_PM"], NX * s + x)
                    nc.vector.tensor_copy(seen[:], ones[:])
                    nc.vector.copy_predicated(right(PM[:], size), together(half_mask[:, x], size).bitcast(U32),
                                              together(UL[:, x], size)).then_inc(S["dve_PM"], 1)
            dve.wait_ge(S["dve_PM"], NX * s + NL)
            nc.vector.tensor_copy(seen[:], ones[:])
            nc.vector.copy_predicated(PM[:], base_mask.bitcast(U32), UB[:, 0]).then_inc(S["dve_PM"], 1)

        def pool_taps(pool, h, hp):
            after(pool, S["dve_silu"], NP * (h - 1))
            nc.gpsimd.tensor_copy(taps[:, hp].unsqueeze(1), taps_all[:, bass.ds(h, 1)]).then_inc(S["taps_set"], 1)

        def pool_newton(pool, h, hp):
            pool.wait_ge(S["dve_ss"], h + 1)
            k = 12 * h
            y = nwt[:, 0]
            for it in range(3):
                dst = (nwt[:, 3], nwt[:, 4], nwt[:, 3])[it]
                nc.gpsimd.tensor_tensor(nwt[:, 1], y, y, ALU.mult).then_inc(S["pool_n"], 1)
                pool.wait_ge(S["pool_n"], k + 4 * it + 1)
                nc.gpsimd.tensor_tensor(nwt[:, 2], nwt[:, 1], ss[:, 2], ALU.mult).then_inc(S["pool_n"], 1)
                pool.wait_ge(S["pool_n"], k + 4 * it + 2)
                nc.gpsimd.tensor_tensor(nwt[:, 1], nwt[:, 2], half3[:].broadcast_to([P, TILES]), ALU.add).then_inc(S["pool_n"], 1)
                pool.wait_ge(S["pool_n"], k + 4 * it + 3)
                nc.gpsimd.tensor_tensor(dst, y, nwt[:, 1], ALU.mult).then_inc(S["pool_n"], 1)
                pool.wait_ge(S["pool_n"], k + 4 * it + 4)
                y = dst
            nc.gpsimd.tensor_tensor(c[:, hp].rearrange("p b n -> p (b n)").unsqueeze(2), y.unsqueeze(2),
                                    beta_rows[:, :, bass.ds(h, 1)], ALU.mult).then_inc(S["pool_c"], 1)

        def pool_XT(pool, eh, en, ep, es, st, prologue):
            ee = en % 2
            wt = headT["w"][:, ep, :, en * P:(en + 1) * P]
            pool.wait_ge(S["act_z"], 4 * es + 3)
            if not prologue:
                after(pool, S["pe_P"], es - 1)
            nc.gpsimd.tensor_tensor(XT[:, ee, BM], FT[:, ee, BM], wt, ALU.mult)
            for x, size in enumerate(LEVELS):
                last = nc.gpsimd.tensor_tensor(left(XT[:, ee, 1 + x], size), left(FT[:, ee, 1 + x], size), left(wt, size), ALU.mult)
            last.then_inc(S["pool_XT"], 1)

        def pool_end(pool, en, es, st, prologue):
            pool.wait_ge(S["act_z"], 4 * es + 4)
            pool.wait_ge(S["act_w"], es + 1)
            if not prologue:
                after(pool, S["pe_St"], st)
            nc.gpsimd.tensor_tensor(Xend[:, en % 2], Fend[:], wR[:], ALU.mult).then_inc(S["pool_end"], 1)

        def pool_step(pool, h, n, hp, early, ready, piece, last_head):
            taps_too = not (isinstance(h, int) and h + 2 >= H)
            if n == 0 and taps_too:
                pool_taps(pool, h + 2, hp)
            if early:
                pool_XT(pool, *early, False)
                pool_end(pool, early[1], early[3], early[4], False)
            if n == 1 and not last_head:
                pool_newton(pool, h + 1, 1 - hp)
            if n == NC - 1:
                pool.wait_ge(S["act_a"], NC * (h + 1))
                nc.gpsimd.tensor_copy(l_all[:, bass.ds(h, 1), :], l[:, hp].rearrange("p b n -> p (b n)").unsqueeze(1))\
                    .then_inc(S["pool_l"], 1)

        def heads(eng, step):
            def pair(i, last_pair):
                for hp in range(2):
                    h = 2 * i + hp
                    last_head = last_pair and hp == 1
                    for n in range(NC):
                        last_step = n == NC - 1
                        eh, en, ep = (h + 1, 0, 1 - hp) if last_step else (h, n + 1, hp)
                        early = None if last_head and last_step else (eh, en, ep, NC * h + n + 1, (NC - 1) * h + n)
                        ready, piece = [None if last_head or last_pair and n >= NC - lead else
                                        (h + 1, 1 - hp, n + lead) if n + lead < NP else (h + 2, hp, n + lead - NP)
                                        for lead in (1, 2)]
                        step(eng, h, n, hp, early, ready, piece, last_head)
            pair(0, False)
            with eng.Fori(1, H // 2 - 1) as i:
                pair(i, False)
            pair(H // 2 - 1, True)

        first = (0, 0, 0, 0, 0)
        first_pieces = [(0, 0, p) for p in range(NP)] + [(1, 1, 0)]
        next_piece = (1, 1, 1)

        def load_weights(sp, h, hp):
            for j, name in enumerate(names):
                src = w[f"L0_attn_a_W{name}"].rearrange("(k p) n -> p k n", p=P)[:, :, bass.ds(h * D, D)]
                sp.dma_start(weights[:, hp, j], src).then_inc(w_in[hp], 16)

        def load_g(sp, h, hp):
            sp.dma_start(g[:, hp].rearrange("p b n d -> p (b n d)").unsqueeze(1),
                         g_dram.rearrange("h p t m -> p h (t m)")[:, bass.ds(h, 1)]).then_inc(g_in[hp], 16)

        @blk.sync
        def _(sp):
            for j, name in enumerate(("q", "k", "v")):
                sp.dma_start(taps_all[:, :, j, :], w[f"L0_attn_a_c{name}"].rearrange("(h p) k -> p h k", p=P))\
                    .then_inc(S["taps_in"], 16)
            for h in range(2):
                load_weights(sp, h, h)
            load_g(sp, 0, 0)

            def head(h, hp, weights_too, g_too):
                if weights_too:
                    sp.wait_ge(S["pe_proj"], NP * (h + 1))
                    load_weights(sp, h + 2, hp)
                if g_too:
                    after(sp, S["pe_z"], 4 * NC * h)
                    after(sp, S["g_floored"], h)
                    load_g(sp, h + 1, 1 - hp)
                sp.wait_ge(S["act_O"], NC * (h + 1))
                sp.dma_start(o_dram.rearrange("t p c -> p t c")[:, :, bass.ds(h * D, D)],
                             o[:, hp].rearrange("p b n d -> p (b n) d")).then_inc(S["o_out"], 16)
            for hp in range(2):
                head(hp, hp, True, True)
            with sp.Fori(1, H // 2 - 1) as i:
                for hp in range(2):
                    head(2 * i + hp, hp, True, True)
            head(H - 2, 0, False, True)
            head(H - 1, 1, False, False)
            sp.wait_ge(S["o_out"], 16 * H)

        @blk.tensor
        def _(pe):
            pe.wait_ge(S["ones_set"], 1)
            for piece in first_pieces:
                pe_project(pe, *piece)
                if piece == (0, 0, 1):
                    pe_sumsq(pe, 0)
            pe_early(pe, *first, True)
            pe_sums(pe, *first[:4], range(4), len(first_pieces))
            pe_XR(pe, 0, 0)
            pe.wait_ge(S["act_XR"], 1)
            pe_project(pe, *next_piece)
            heads(pe, pe_step)

        @blk.scalar
        def _(act):
            for piece in first_pieces:
                act_piece(act, *piece)
                act_tanh(act, *piece)
                act_sq(act, *piece)
            act_rows(act, *first, True)
            act_factors(act, 0, 0, range(3))
            act_end(act, 0, True)
            act_XR(act, 0, 0, 0, True)
            act_piece(act, *next_piece)
            heads(act, act_step)

        @blk.vector
        def _(dve):
            nc.vector.memset(ones[:], 1.0).then_inc(S["ones_set"], 1)
            nc.vector.memset(half3[:], 1.5).then_inc(S["half3_set"], 1)
            nc.vector.memset(XT[:], 0.0).then_inc(S["zeros_set"], 1)
            nc.vector.memset(PT[:], 0.0).then_inc(S["zeros_set"], 1)
            nc.vector.memset(PM[:], 0.0).then_inc(S["zeros_set"], 1)
            dve.wait_ge(S["taps_in"], 48)
            nc.vector.tensor_scalar(taps_all[:], taps_all[:], 0.5, None, ALU.mult).then_inc(S["taps_halved"], 1)
            for piece in first_pieces:
                dve_conv(dve, *piece, range(1, KW))
                dve_silu(dve, *piece)
                if piece == (0, 0, 1):
                    dve_sumsq(dve, 0)
            dve_floor(dve, 0, 0)
            dve_A(dve, 0)
            dve.wait_ge(S["zeros_set"], 3)
            heads(dve, dve_step)

        @blk.gpsimd
        def _(pool):
            pool.wait_ge(S["taps_halved"], 1)
            pool.wait_ge(S["half3_set"], 1)
            pool.wait_ge(S["zeros_set"], 3)
            for h in range(2):
                pool_taps(pool, h, h)
            pool_newton(pool, 0, 0)
            pool_XT(pool, *first, True)
            pool_end(pool, 0, 0, 0, True)
            heads(pool, pool_step)
            pool.wait_ge(S["pool_l"], H)


def gated_output(nc, x, hT, w, ident, o_dram, l_all, loads):
    G = 4
    with Phase(nc, "gate") as ph:
        wg1 = ph.sb("wg1", [P, KC, D])
        wg2 = ph.sb("wg2", [P, H * D])
        bg2 = ph.sb("bg2", [1, H * D])
        norm_w = ph.sb("norm_w", [D, 1])
        wo = ph.sb("wo", [D, H, HID])
        ones = ph.sb("ones", [1, P])
        el2 = ph.sb("el2", [P, H, TILES])
        o = ph.sb("o", [P, 2, H, D])
        sq = ph.sb("sq", [P, H, D])
        ss = ph.sb("ss", [P, H])
        ms = ph.sb("ms", [P, H])
        rms = ph.sb("rms", [P, H])
        rrms = ph.sb("rrms", [P, H])
        f = ph.sb("f", [P, 2, P])
        th = ph.sb("th", [P, H, D])
        og = ph.sb("og", [P, H, D])
        y = ph.sb("y", [P, 2, H, D])
        yT = ph.sb("yT", [P, 2, H, P])
        ps_gate = ph.ps("ps_gate", [P, H, D])
        ps_turn = ph.ps("ps_turn", [P, 2, G, P])
        ps_f = ph.ps("ps_f", [P, 512])
        ps_out = ph.ps("ps_out", [P, 512])
        S = {n: ph.sem(n) for n in ("loaded w_in ones_set wo_scaled el2_ready sq ss ms rms rrms f_raw f gate th og y turned "
                                    "yT out x").split()}
        o_in = [ph.sem(f"o_in{n}") for n in range(2)]
        blk = ph.block()

        @blk.sync
        def _(sp):
            sp.dma_start(wg1[:], w["L0_attn_a_Wg1"].rearrange("(k p) n -> p k n", p=P)).then_inc(S["w_in"], 16)
            sp.dma_start(wg2[:], w["L0_attn_a_Wg2"]).then_inc(S["w_in"], 16)
            sp.dma_start(bg2[:], w["L0_attn_a_bg2"].rearrange("(a n) -> a n", a=1)).then_inc(S["w_in"], 16)
            sp.dma_start(norm_w[:], w["L0_attn_a_norm_w"].rearrange("(p a) -> p a", a=1)).then_inc(S["w_in"], 16)
            sp.dma_start(wo[:], w["L0_attn_a_Wo"].rearrange("(h p) n -> p h n", p=P)).then_inc(S["w_in"], 16)

            def tile(t, par):
                after(sp, S["og"], t - 1)
                sp.dma_start(o[:, par].rearrange("p h d -> p (h d)").unsqueeze(1),
                             o_dram.rearrange("t p c -> p t c")[:, bass.ds(t, 1)]).then_inc(o_in[par], 16)
            for t in range(2):
                tile(t, t)
            for dst, src in loads:
                sp.dma_start(dst, src).then_inc(S["loaded"], 16)
            with sp.Fori(1, TILES // 2) as i:
                for par in range(2):
                    tile(2 * i + par, par)
            sp.wait_ge(S["loaded"], 16 * len(loads))

        @blk.tensor
        def _(pe):
            pe.wait_ge(S["w_in"], 80)
            pe.wait_ge(S["ones_set"], 1)

            def gate(t, par):
                after(pe, S["f"], t)
                for k in range(KC):
                    last = nc.tensor.matmul(ps_f[:, 0:P], wg1[:, k, :], hT[:, k, bass.ds(t * P, P)],
                                            start=k == 0, stop=k == KC - 1)
                last.then_inc(S["f_raw"], 1)
                pe.wait_ge(S["f"], t + 1)
                after(pe, S["th"], t)
                for q in range(H // G):
                    dst = ps_gate[:, q * G:(q + 1) * G, :]
                    nc.tensor.matmul(dst, f[:, par, :], wg2[:, q * 512:(q + 1) * 512], start=True, stop=False)
                    last = nc.tensor.matmul(dst, ones[:], bg2[:, q * 512:(q + 1) * 512], start=False, stop=True)
                last.then_inc(S["gate"], 1)

            def step(t, par, after_it):
                if after_it:
                    gate(t + 1, 1 - par)
                pe.wait_ge(S["y"], t + 1)
                for q in range(H // G):
                    after(pe, S["yT"], H // G * t + q - 1)
                    for j in range(G):
                        last = nc.tensor.transpose(ps_turn[:, q % 2, j, :], y[:, par, q * G + j, :], ident)
                    last.then_inc(S["turned"], 1)
                pe.wait_ge(S["yT"], H // G * (t + 1))
                pe.wait_ge(S["wo_scaled"], 1)
                after(pe, S["x"], t)
                for h in range(H):
                    last = nc.tensor.matmul(ps_out[:, 0:HID], yT[:, par, h, :], wo[:, h, :], start=h == 0, stop=h == H - 1)
                last.then_inc(S["out"], 1)
            gate(0, 0)
            by_tiles_ahead(pe, step)

        @blk.scalar
        def _(act):
            def make(t, par):
                act.wait_ge(S["f_raw"], t + 1)
                nc.scalar.activation(f[:, par], ps_f[:, 0:P], ACT.Copy).then_inc(S["f"], 1)
                act.wait_ge(o_in[par], 8 * (t - par) + 16)
                after(act, S["ss"], t)
                nc.scalar.activation(sq[:], o[:, par], ACT.Square).then_inc(S["sq"], 1)
                act.wait_ge(S["gate"], t + 1)
                after(act, S["og"], t)
                nc.scalar.activation(th[:], ps_gate[:], ACT.Tanh, scale=0.5).then_inc(S["th"], 1)
                act.wait_ge(S["ms"], t + 1)
                nc.scalar.activation(rms[:], ms[:], ACT.Sqrt).then_inc(S["rms"], 1)

            def step(t, par, after_it):
                if after_it:
                    make(t + 1, 1 - par)
                for q in range(H // G):
                    act.wait_ge(S["turned"], H // G * t + q + 1)
                    nc.scalar.activation(yT[:, par, q * G:(q + 1) * G, :], ps_turn[:, q % 2], ACT.Copy).then_inc(S["yT"], 1)
            make(0, 0)
            by_tiles_ahead(act, step)

        @blk.vector
        def _(dve):
            nc.vector.memset(ones[:], 1.0).then_inc(S["ones_set"], 1)
            dve.wait_ge(S["w_in"], 80)
            nc.vector.tensor_scalar(wo[:], wo[:], norm_w[:, 0:1], 0.5, ALU.mult, ALU.mult).then_inc(S["wo_scaled"], 1)
            nc.vector.scalar_tensor_tensor(el2[:], l_all[:], EPS, l_all[:], ALU.mult, ALU.mult).then_inc(S["el2_ready"], 1)
            dve.wait_ge(S["el2_ready"], 1)

            def make(t, par):
                dve.wait_ge(S["sq"], t + 1)
                nc.vector.tensor_reduce(ss[:], sq[:], X, ALU.add).then_inc(S["ss"], 1)
                dve.wait_ge(S["ss"], t + 1)
                nc.vector.scalar_tensor_tensor(ms[:].unsqueeze(2), ss[:].unsqueeze(2), 1.0 / D, el2[:, :, bass.ds(t, 1)],
                                               ALU.mult, ALU.add).then_inc(S["ms"], 1)
                dve.wait_ge(S["th"], t + 1)
                nc.vector.scalar_tensor_tensor(og[:], th[:], 1.0, o[:, par], ALU.add, ALU.mult).then_inc(S["og"], 1)
                dve.wait_ge(S["rms"], t + 1)
                nc.vector.reciprocal(rrms[:], rms[:]).then_inc(S["rrms"], 1)
                dve.wait_ge(S["rrms"], t + 1)
                after(dve, S["turned"], H // G * (t - 1))
                dve.wait_ge(S["og"], t + 1)
                nc.vector.tensor_tensor(y[:, par], og[:], rrms[:].unsqueeze(2).broadcast_to([P, H, D]), ALU.mult)\
                    .then_inc(S["y"], 1)

            def step(t, par, after_it):
                if after_it:
                    make(t + 1, 1 - par)
                dve.wait_ge(S["out"], t + 1)
                nc.vector.tensor_tensor(x[:, bass.ds(t, 1)], x[:, bass.ds(t, 1)], ps_out[:, 0:HID].unsqueeze(1), ALU.add)\
                    .then_inc(S["x"], 1)
            make(0, 0)
            by_tiles_ahead(dve, step)
            dve.wait_ge(S["x"], TILES)


def experts(nc, name, x, hT, W, consts):
    ident, before = consts["ident"], consts["before"]
    NQ = 4
    EQ = NE // NQ
    CH = NE * EH // P
    CQ = CH // NQ
    with Phase(nc, name) as ph:
        hc = ph.sb("hc", [P, 2, KC, P])
        scores = ph.sb("scores", [P, NE + 2])
        th = ph.sb("th", [P, NE])
        top = ph.sb("top", [P, 8])
        left = ph.sb("left", [P, NE + 2])
        sel = ph.sb("sel", [P, NE])
        seen = ph.sb("seen", [P, NE])
        wsel = ph.sb("wsel", [P, NE])
        wsum = ph.sb("wsum", [P, 1])
        rsum = ph.sb("rsum", [P, 1])
        wcap = ph.sb("wcap", [P, NE])
        comb = ph.sb("comb", [P, 2, NE])
        ones = ph.sb("ones", [P, P])
        ths = ph.sb("ths", [P, SH])
        gs = ph.sb("gs", [P, SH])
        hs = ph.sb("hs", [P, 2, SH])
        hsT = ph.sb("hsT", [SH, 2, P])
        tg = ph.sb("tg", [P, 2, EQ, EH])
        sg = ph.sb("sg", [P, EQ, EH])
        vw = ph.sb("vw", [P, EQ, EH])
        r = ph.sb("r", [P, 2, EQ, EH])
        rT = ph.sb("rT", [P, 2, CH, P])
        ps_up = ph.ps("ps_up", [P, 2, EQ, 2 * EH])
        ps_turn = ph.ps("ps_turn", [P, 2, CQ, P])
        ps_g = ph.ps("ps_g", [P, 512])
        ps_out = ph.ps("ps_out", [P, 512])
        S = {n: ph.sem(n) for n in ("set hc g th ths sc top left sel wsel wsum rsum pos wcap comb seen gs hs up tg sg vw r "
                                    "turned rT hsturned hsT out x").split()}
        blk = ph.block()
        Z, SU, POS = slice(0, NE), slice(NE, NE + 2 * SH), slice(NE + 2 * SH, 2 * NE + 2 * SH)
        TURN = slice(2 * NE + 2 * SH, 2 * NE + 2 * SH + P)

        def steps(eng, step):
            for t in range(2):
                step(eng, t, t, t > 0, True)
            with eng.Fori(1, TILES // 2 - 1) as i:
                for par in range(2):
                    step(eng, 2 * i + par, par, True, True)
            for par in range(2):
                step(eng, TILES - 2 + par, par, True, par == 0)

        def pe_gate(pe, t, par):
            pe.wait_ge(S["hc"], t + 1)
            after(pe, S["hsT"], t)
            for k in range(KC):
                nc.tensor.matmul(ps_g[:, Z], hc[:, par, k], W["gate"][:, k], start=k == 0, stop=k == KC - 1)
            for k in range(KC):
                last = nc.tensor.matmul(ps_g[:, SU], hc[:, par, k], W["shared_up"][:, k], start=k == 0, stop=k == KC - 1)
            last.then_inc(S["g"], 1)

        def pe_position(pe, t):
            pe.wait_ge(S["seen"], t + 1)
            pe.wait_ge(S["hs"], t + 1)
            nc.tensor.matmul(ps_g[:, POS], before, sel[:], start=True, stop=False)
            nc.tensor.matmul(ps_g[:, POS], ones[:], seen[:], start=False, stop=True).then_inc(S["pos"], 1)

        def pe_turn_shared(pe, t, par):
            nc.tensor.transpose(ps_g[0:SH, TURN], hs[:, par], ident).then_inc(S["hsturned"], 1)

        def pe_up(pe, t, par, q):
            after(pe, S["vw"], NQ * t + q - 1)
            for c in range(2):
                for k in range(KC):
                    last = nc.tensor.matmul(ps_up[:, q % 2, c * EQ // 2:(c + 1) * EQ // 2, :], hc[:, par, k],
                                            W["up"][:, k, q * EQ + c * EQ // 2:q * EQ + (c + 1) * EQ // 2, :],
                                            start=k == 0, stop=k == KC - 1)
            last.then_inc(S["up"], 1)

        def pe_turn(pe, t, q):
            pe.wait_ge(S["r"], NQ * t + q + 1)
            after(pe, S["rT"], NQ * t + q - 1)
            for c in range(CQ):
                last = nc.tensor.transpose(ps_turn[:, q % 2, c, :],
                                           r[:, q % 2].rearrange("p e h -> p (e h)")[:, c * P:(c + 1) * P], ident)
            last.then_inc(S["turned"], 1)

        def pe_down(pe, t, par):
            pe.wait_ge(S["rT"], NQ * (t + 1))
            after(pe, S["x"], t)
            for c in range(CH):
                nc.tensor.matmul(ps_out[:, 0:HID], rT[:, par, c], W["down"][:, c], start=c == 0, stop=False)
            nc.tensor.matmul(ps_out[:, 0:HID], hsT[:, par], W["shared_down"][:], start=False, stop=True).then_inc(S["out"], 1)

        def pe_step(pe, t, par, before_it, after_it):
            pe_up(pe, t, par, 0)
            if before_it:
                pe_turn(pe, t - 1, NQ - 1)
            if after_it:
                pe_gate(pe, t + 1, 1 - par)
            pe_up(pe, t, par, 1)
            if before_it:
                pe_down(pe, t - 1, 1 - par)
            pe_up(pe, t, par, 2)
            pe_turn(pe, t, 0)
            if after_it:
                pe_position(pe, t + 1)
            pe_up(pe, t, par, 3)
            if after_it:
                pe.wait_ge(S["wcap"], t + 2)
            pe_turn(pe, t, 1)
            if after_it:
                pe_turn_shared(pe, t + 1, 1 - par)
            pe_turn(pe, t, 2)

        @blk.tensor
        def _(pe):
            pe.wait_ge(S["set"], 3)
            pe_gate(pe, 0, 0)
            pe_position(pe, 0)
            pe.wait_ge(S["wcap"], 1)
            pe_turn_shared(pe, 0, 0)
            steps(pe, pe_step)
            pe_turn(pe, TILES - 1, NQ - 1)
            pe_down(pe, TILES - 1, 1)

        def act_tile(act, t, par):
            after(act, S["up"], NQ * (t - 1))
            nc.scalar.activation(hc[:, par], hT[:, :, bass.ds(t * P, P)], ACT.Copy).then_inc(S["hc"], 1)

        def act_gate(act, t):
            act.wait_ge(S["g"], t + 1)
            after(act, S["hs"], t)
            nc.scalar.activation(th[:], ps_g[:, Z], ACT.Tanh, scale=0.5).then_inc(S["th"], 1)
            nc.scalar.activation(ths[:], ps_g[:, NE + SH:NE + 2 * SH], ACT.Tanh, scale=0.5).then_inc(S["ths"], 1)

        def act_up(act, t, q):
            act.wait_ge(S["up"], NQ * t + q + 1)
            after(act, S["sg"], NQ * t + q - 1)
            nc.scalar.activation(tg[:, q % 2], ps_up[:, q % 2, :, 0:EH], ACT.Tanh, scale=0.5).then_inc(S["tg"], 1)

        def act_r(act, t, par, q):
            act.wait_ge(S["turned"], NQ * t + q + 1)
            nc.scalar.activation(rT[:, par, q * CQ:(q + 1) * CQ], ps_turn[:, q % 2], ACT.Copy).then_inc(S["rT"], 1)

        def act_shared(act, t, par):
            act.wait_ge(S["hsturned"], t + 1)
            nc.scalar.activation(hsT[:, par], ps_g[0:SH, TURN], ACT.Copy).then_inc(S["hsT"], 1)

        def act_step(act, t, par, before_it, after_it):
            if after_it:
                act_tile(act, t + 1, 1 - par)
            act_up(act, t, 0)
            if before_it:
                act_r(act, t - 1, 1 - par, NQ - 1)
            if after_it:
                act_gate(act, t + 1)
            act_up(act, t, 1)
            act_up(act, t, 2)
            act_r(act, t, par, 0)
            act_up(act, t, 3)
            act_r(act, t, par, 1)
            if after_it:
                act_shared(act, t + 1, 1 - par)
            act_r(act, t, par, 2)

        @blk.scalar
        def _(act):
            act_tile(act, 0, 0)
            act_gate(act, 0)
            act_shared(act, 0, 0)
            steps(act, act_step)
            act_r(act, TILES - 1, 1, NQ - 1)

        def dve_choose(dve, t, par):
            dve.wait_ge(S["th"], t + 1)
            nc.vector.tensor_scalar(scores[:, 0:NE], th[:], 0.5, 0.5, ALU.mult, ALU.add).then_inc(S["sc"], 1)
            dve.wait_ge(S["sc"], t + 1)
            if not (isinstance(t, int) and t == 0):
                dve.wait_ge(S["pos"], t)
                nc.vector.tensor_tensor(seen[:], seen[:], sel[:], ALU.add)
            nc.vector.max(top[:], scores[:]).then_inc(S["top"], 1)
            dve.wait_ge(S["ths"], t + 1)
            dve.wait_ge(S["top"], t + 1)
            nc.vector.scalar_tensor_tensor(gs[:], ths[:], 1.0, ps_g[:, NE + SH:NE + 2 * SH], ALU.add, ALU.mult)\
                .then_inc(S["gs"], 1)
            nc.vector.match_replace(left[:], top[:], scores[:], -1.0).then_inc(S["left"], 1)
            dve.wait_ge(S["left"], t + 1)
            nc.vector.tensor_scalar(sel[:], left[:, 0:NE], 0.0, None, ALU.is_lt).then_inc(S["seen"], 1)
            dve.wait_ge(S["gs"], t + 1)
            nc.vector.scalar_tensor_tensor(hs[:, par], gs[:], 0.5, ps_g[:, NE:NE + SH], ALU.mult, ALU.mult)\
                .then_inc(S["hs"], 1)
            dve.wait_ge(S["seen"], t + 1)
            nc.vector.tensor_tensor(wsel[:], sel[:], scores[:, 0:NE], ALU.mult).then_inc(S["wsel"], 1)
            dve.wait_ge(S["wsel"], t + 1)
            nc.vector.tensor_reduce(wsum[:], wsel[:], X, ALU.add).then_inc(S["wsum"], 1)
            dve.wait_ge(S["wsum"], t + 1)
            nc.vector.reciprocal(rsum[:], wsum[:]).then_inc(S["rsum"], 1)

        def dve_weigh(dve, t, par):
            dve.wait_ge(S["pos"], t + 1)
            nc.vector.scalar_tensor_tensor(wcap[:], ps_g[:, POS], float(CAP), wsel[:], ALU.is_lt, ALU.mult)\
                .then_inc(S["wcap"], 1)
            dve.wait_ge(S["wcap"], t + 1)
            dve.wait_ge(S["rsum"], t + 1)
            nc.vector.tensor_scalar(comb[:, par], wcap[:], rsum[:, 0:1], 0.5, ALU.mult, ALU.mult).then_inc(S["comb"], 1)

        def dve_hidden(dve, t, par, q):
            after(dve, S["r"], NQ * t + q)
            dve.wait_ge(S["tg"], NQ * t + q + 1)
            nc.vector.scalar_tensor_tensor(sg[:], tg[:, q % 2], 1.0, ps_up[:, q % 2, :, 0:EH], ALU.add, ALU.mult)\
                .then_inc(S["sg"], 1)
            if q == 0:
                dve.wait_ge(S["comb"], t + 1)
            nc.vector.tensor_tensor(vw[:], ps_up[:, q % 2, :, EH:2 * EH],
                                    comb[:, par, q * EQ:(q + 1) * EQ].unsqueeze(2).broadcast_to([P, EQ, EH]),
                                    ALU.mult).then_inc(S["vw"], 1)
            after(dve, S["turned"], NQ * t + q - 1)
            dve.wait_ge(S["vw"], NQ * t + q + 1)
            nc.vector.tensor_tensor(r[:, q % 2], sg[:], vw[:], ALU.mult).then_inc(S["r"], 1)

        def dve_out(dve, t):
            dve.wait_ge(S["out"], t + 1)
            nc.vector.tensor_tensor(x[:, bass.ds(t, 1)], x[:, bass.ds(t, 1)], ps_out[:, 0:HID].unsqueeze(1), ALU.add)\
                .then_inc(S["x"], 1)

        def dve_step(dve, t, par, before_it, after_it):
            dve_hidden(dve, t, par, 0)
            if after_it:
                dve_choose(dve, t + 1, 1 - par)
            dve_hidden(dve, t, par, 1)
            if before_it:
                dve_out(dve, t - 1)
            dve_hidden(dve, t, par, 2)
            if after_it:
                dve_weigh(dve, t + 1, 1 - par)
            dve_hidden(dve, t, par, 3)

        @blk.vector
        def _(dve):
            nc.vector.memset(ones[:], 1.0).then_inc(S["set"], 1)
            nc.vector.memset(seen[:], 0.0).then_inc(S["set"], 1)
            nc.vector.memset(scores[:, NE:NE + 2], 2.0).then_inc(S["set"], 1)
            dve.wait_ge(S["set"], 3)
            dve_choose(dve, 0, 0)
            dve_weigh(dve, 0, 0)
            steps(dve, dve_step)
            dve_out(dve, TILES - 1)
            dve.wait_ge(S["x"], TILES)


def linear_attention(nc, x, hT, w, consts):
    C = BH * BD
    with Phase(nc, "lin") as keep:
        wout = keep.sb("wout", [P, KC, C])
        kT = keep.sb("kT", [P, KC, TILES * P])
        rT = keep.sb("rT", [P, KC, TILES * P])
        kv = keep.sb("kv", [P, TILES, 2, C])
        g = keep.sb("g", [P, TILES, C])
        gf = keep.sb("gf", [P, TILES, C])
        ps = keep.ps("ps", [P, 8, 512])
        linear_inputs(nc, hT, w, wout, kT, rT, kv, g, gf, ps)
        linear_chunks(nc, x, wout, kT, rT, kv, g, gf, ps, consts)


def linear_inputs(nc, hT, w, wout, kT, rT, kv, g, gf, ps):
    C = BH * BD
    with Phase(nc, "lin_in") as ph:
        W = {n: ph.sb(f"W{n}", [P, KC, C]) for n in ("x", "w", "r", "k")} | {"out": wout}
        Wkv = ph.sb("Wkv", [P, KC, 2, C])
        bw = ph.sb("bw", [1, C])
        ones = ph.sb("ones", [1, P])
        uT = ph.sb("uT", [P, KC, TILES * P])
        rth = ph.sb("rth", [P, KC, TILES * P])
        ab = ph.sb("ab", [P, TILES, C])
        ex = ph.sb("ex", [P, TILES, C])
        ln = ph.sb("ln", [P, TILES, C])
        S = {n: ph.sem(n) for n in "w_in ones_set pu u pk pr k rth r pkv kv pz ab ex ln gz g gf".split()}
        blk = ph.block()
        NH = TILES * P // 512

        @blk.sync
        def _(sp):
            for n in ("x", "w", "r", "k", "out"):
                sp.dma_start(W[n][:], w[f"L0_attn_b_W{n}"].rearrange("(k p) n -> p k n", p=P)).then_inc(S["w_in"], 16)
            for j, n in enumerate(("k", "v")):
                sp.dma_start(Wkv[:, :, j], w[f"L0_attn_b_W{n}"].rearrange("(k p) n -> p k n", p=P)).then_inc(S["w_in"], 16)
            sp.dma_start(bw[:], w["L0_attn_b_bw"].rearrange("(a n) -> a n", a=1)).then_inc(S["w_in"], 16)

        def project(weight, first_bank):
            for half in range(KC):
                for c in range(NH):
                    for k in range(KC):
                        last = nc.tensor.matmul(ps[:, first_bank + half * NH + c], weight[:, k, half * P:(half + 1) * P],
                                                hT[:, k, c * 512:(c + 1) * 512], start=k == 0, stop=k == KC - 1)
            return last

        def banks(first):
            return ps[:, first:first + KC * NH].rearrange("p (k c) t -> p k (c t)", k=KC)

        @blk.tensor
        def _(pe):
            pe.wait_ge(S["w_in"], 128)
            pe.wait_ge(S["ones_set"], 1)
            project(W["x"], 0).then_inc(S["pu"], 1)
            project(W["k"], 4).then_inc(S["pk"], 1)
            pe.wait_ge(S["u"], 1)
            for t in range(TILES):
                dst = ps[:, t // 2, t % 2 * C:(t % 2 + 1) * C]
                for k in range(KC):
                    nc.tensor.matmul(dst, uT[:, k, t * P:(t + 1) * P], W["w"][:, k], start=k == 0, stop=False)
                last = nc.tensor.matmul(dst, ones[:], bw[:], start=False, stop=True)
            last.then_inc(S["pz"], 1)
            pe.wait_ge(S["k"], 1)
            project(W["r"], 4).then_inc(S["pr"], 1)
            pe.wait_ge(S["gz"], 1)
            for t in range(TILES):
                if t == 4:
                    pe.wait_ge(S["rth"], 1)
                for k in range(KC):
                    last = nc.tensor.matmul(ps[:, t], hT[:, k, t * P:(t + 1) * P], Wkv[:, k], start=k == 0, stop=k == KC - 1)
                last.then_inc(S["pkv"], 1)

        @blk.scalar
        def _(act):
            act.wait_ge(S["pu"], 1)
            nc.scalar.activation(uT[:], banks(0), ACT.Copy).then_inc(S["u"], 1)
            act.wait_ge(S["pz"], 1)
            z = ps[:, 0:4].rearrange("p a (b c) -> p (a b) c", b=2)
            nc.scalar.activation(ab[:], z, ACT.Abs).then_inc(S["ab"], 1)
            act.wait_ge(S["ab"], 1)
            nc.scalar.activation(ex[:], ab[:], ACT.Exp, scale=-1.0).then_inc(S["ex"], 1)
            act.wait_ge(S["ex"], 1)
            nc.scalar.activation(ln[:], ex[:], ACT.Ln, bias=1.0).then_inc(S["ln"], 1)
            act.wait_ge(S["pr"], 1)
            nc.scalar.activation(rth[:], banks(4), ACT.Tanh, scale=0.5).then_inc(S["rth"], 1)
            for t in range(TILES):
                act.wait_ge(S["pkv"], t + 1)
                nc.scalar.activation(kv[:, t], ps[:, t].rearrange("p (j c) -> p j c", j=2), ACT.Copy).then_inc(S["kv"], 1)
            act.wait_ge(S["kv"], TILES)

        @blk.vector
        def _(dve):
            nc.vector.memset(ones[:], 1.0).then_inc(S["ones_set"], 1)
            dve.wait_ge(S["pk"], 1)
            nc.vector.tensor_copy(kT[:], banks(4)).then_inc(S["k"], 1)
            dve.wait_ge(S["ln"], 1)
            z = ps[:, 0:4].rearrange("p a (b c) -> p (a b c)", b=2)
            nc.vector.scalar_tensor_tensor(ab[:].rearrange("p t c -> p (t c)"), z, 0.0, ln[:].rearrange("p t c -> p (t c)"),
                                           ALU.max, ALU.add).then_inc(S["gz"], 1)
            dve.wait_ge(S["gz"], 1)
            nc.vector.tensor_scalar(g[:], ab[:], -1.0, None, ALU.mult).then_inc(S["g"], 1)
            nc.vector.tensor_scalar(gf[:], ab[:], -1.0, -FLOOR, ALU.mult, ALU.max).then_inc(S["gf"], 1)
            dve.wait_ge(S["rth"], 1)
            nc.vector.tensor_scalar(rT[:], rth[:], 0.5, 0.5, ALU.mult, ALU.add).then_inc(S["r"], 1)
            dve.wait_ge(S["r"], 1)
            dve.wait_ge(S["g"], 1)
            dve.wait_ge(S["gf"], 1)


def linear_chunks(nc, x, wout, kT, rT, kv, g, gf, ps, consts):
    sums, mask, ident = consts["sums"], consts["mask"], consts["ident"]
    NX = NL + 1
    C = BH * BD
    RING = 6
    UNITS = NX * 2
    with Phase(nc, "chunks") as ph:
        F = ph.sb("F", [P, NX + 2, KC, B, P])
        Fend = ph.sb("Fend", [P, B, C])
        XT = ph.sb("XT", [P, NX, KC, B, P])
        EF = ph.sb("EF", [P, NX + 1, KC, B, P])
        Xend = ph.sb("Xend", [P, 2, B, C])
        PM = ph.sb("PM", [P, 2, KC, B, P])
        St = ph.sb("St", [P, 2, KC, B, P])
        y = ph.sb("y", [P, B, C])
        yT = ph.sb("yT", [P, B, KC, P])
        S = {n: ph.sem(n) for n in "zero z F XT EF Xend P PM st St o y yt yT out x".split()}
        blk = ph.block()
        bank_o, bank_s = ps[:, 6], ps[:, 7]

        def kT_of(T_, n):
            return T_[:].rearrange("p k (b t) -> p k b t", b=B)[:, :, :, n * P:(n + 1) * P]

        @blk.tensor
        def _(pe):
            def levels(n):
                if n:
                    pe.wait_ge(S["PM"], UNITS * n)
                for z in range(NX + 1):
                    gz = gf if z == BASE else g
                    for k in range(KC):
                        for b in range(B):
                            last = nc.tensor.matmul(ps[:, z, (k * B + b) * P:(k * B + b + 1) * P],
                                                    gz[:, b * NC + n, k * P:(k + 1) * P], sums[:, z], start=True, stop=True)
                    last.then_inc(S["z"], 1)

            def end(n):
                if n:
                    pe.wait_ge(S["y"], n)
                for b in range(B):
                    last = nc.tensor.matmul(bank_o[:, b * C:(b + 1) * C], sums[:, END], g[:, b * NC + n], start=True, stop=True)
                last.then_inc(S["z"], 1)

            pe.wait_ge(S["zero"], 1)
            levels(0)
            end(0)
            for n in range(NC):
                pe.wait_ge(S["EF"], n + 1)
                pe.wait_ge(S["F"], (NX + 2) * n + NX + 1)
                for u in range(UNITS):
                    xl, half = u // 2, u % 2
                    at = half * BD
                    place = xl + 1 if xl < NL else BASE
                    if u >= RING:
                        pe.wait_ge(S["PM"], UNITS * n + u - RING + 1)
                    for k in range(KC):
                        for b in range(B):
                            last = nc.tensor.matmul(ps[:, u % RING, (k * B + b) * P:(k * B + b + 1) * P],
                                                    XT[at:at + BD, place, k, b], EF[at:at + BD, xl, k, b],
                                                    start=True, stop=True)
                    last.then_inc(S["P"], 1)
                    if u == RING - 1 and n < NC - 1:
                        pe.wait_ge(S["Xend"], n + 1)
                        if n:
                            pe.wait_ge(S["x"], 2 * n)
                        for k in range(KC):
                            for b in range(B):
                                last = nc.tensor.matmul(bank_s[:, (k * B + b) * P:(k * B + b + 1) * P],
                                                        Xend[:, n % 2, b, k * P:(k + 1) * P],
                                                        kv[:, b * NC + n, 1, k * P:(k + 1) * P], start=True, stop=True)
                        last.then_inc(S["st"], 1)
                if n < NC - 1:
                    levels(n + 1)
                pe.wait_ge(S["PM"], UNITS * (n + 1))
                pe.wait_ge(S["F"], (NX + 2) * (n + 1))
                for b in range(B):
                    for k in range(KC):
                        dst = bank_o[:, b * C + k * P:b * C + (k + 1) * P]
                        if n:
                            pe.wait_ge(S["St"], n)
                            nc.tensor.matmul(dst, EF[:, NX, k, b], St[:, (n - 1) % 2, k, b], start=True, stop=False)
                        for half in range(2):
                            last = nc.tensor.matmul(dst[:, half * BD:(half + 1) * BD], PM[:, half, k, b],
                                                    kv[:, b * NC + n, 1, k * P + half * BD:k * P + (half + 1) * BD],
                                                    start=n == 0, stop=n == 0 or half == 1)
                last.then_inc(S["o"], 1)
                if n < NC - 1:
                    end(n + 1)
                pe.wait_ge(S["y"], n + 1)
                pe.wait_ge(S["St"], min(n + 1, NC - 1))
                for b in range(B):
                    for k in range(KC):
                        last = nc.tensor.transpose(bank_s[:, (b * KC + k) * P:(b * KC + k + 1) * P], y[:, b, k * P:(k + 1) * P], ident)
                last.then_inc(S["yt"], 1)
                pe.wait_ge(S["yT"], n + 1)
                for b in range(B):
                    for k in range(KC):
                        last = nc.tensor.matmul(bank_s[:, b * C:(b + 1) * C], yT[:, b, k], wout[:, k], start=k == 0, stop=k == KC - 1)
                last.then_inc(S["out"], 1)

        @blk.scalar
        def _(act):
            for n in range(NC + 1):
                if 0 < n < NC:
                    act.wait_ge(S["EF"], n)
                    act.wait_ge(S["St"], n)
                if n < NC:
                    for z in range(NX + 1):
                        act.wait_ge(S["z"], (NX + 2) * n + z + 1)
                        src = ps[:, z].rearrange("p (k b t) -> p k b t", k=KC, b=B)
                        if z == BASE:
                            nc.scalar.activation(F[:, 0], src, ACT.Exp, scale=-1.0)
                            nc.scalar.activation(F[:, NX], src, ACT.Exp).then_inc(S["F"], 1)
                        else:
                            nc.scalar.activation(F[:, z if z <= NL else NX + 1], src, ACT.Exp).then_inc(S["F"], 1)
                if n:
                    act.wait_ge(S["o"], n)
                    if n > 1:
                        act.wait_ge(S["yt"], n - 1)
                    nc.scalar.activation(y[:], bank_o.rearrange("p (b c) -> p b c", b=B), ACT.Copy).then_inc(S["y"], 1)
                if n < NC:
                    act.wait_ge(S["z"], (NX + 2) * (n + 1))
                    if n:
                        act.wait_ge(S["Xend"], n)
                    nc.scalar.activation(Fend[:], bank_o.rearrange("p (b c) -> p b c", b=B), ACT.Exp).then_inc(S["F"], 1)
                if n:
                    act.wait_ge(S["yt"], n)
                    if n > 1:
                        act.wait_ge(S["out"], n - 1)
                    nc.scalar.activation(yT[:].rearrange("p b k t -> p (b k t)"), bank_s, ACT.Copy).then_inc(S["yT"], 1)

        @blk.vector
        def _(dve):
            nc.vector.memset(St[:], 0.0).then_inc(S["zero"], 1)
            dve.wait_ge(S["zero"], 1)

            def add(n):
                dve.wait_ge(S["out"], n + 1)
                for b in range(B):
                    nc.vector.tensor_tensor(x[:, b * NC + n], x[:, b * NC + n], bank_s[:, b * C:(b + 1) * C], ALU.add)\
                        .then_inc(S["x"], 1)

            for n in range(NC):
                e = n % 2
                src_k, src_r = kT_of(kT, n), kT_of(rT, n)
                dve.wait_ge(S["F"], (NX + 2) * n + NX + 1)
                if n:
                    dve.wait_ge(S["P"], UNITS * n)
                for k in range(KC):
                    nc.vector.tensor_tensor(XT[:, :, k], F[:, 0:NX, k], src_k[:, k].unsqueeze(1).broadcast_to([P, NX, B, P]), ALU.mult)
                if n:
                    dve.wait_ge(S["o"], n)
                for k in range(KC):
                    last = nc.vector.tensor_tensor(EF[:, :, k], F[:, 1:NX + 2, k],
                                                   src_r[:, k].unsqueeze(1).broadcast_to([P, NX + 1, B, P]), ALU.mult)
                last.then_inc(S["EF"], 1)
                dve.wait_ge(S["F"], (NX + 2) * (n + 1))
                nc.vector.tensor_tensor(Xend[:, e], Fend[:], kv[:].rearrange("p (b n) j c -> p b n j c", b=B)[:, :, n, 0],
                                        ALU.mult).then_inc(S["Xend"], 1)
                if n:
                    add(n - 1)
                for u in range(UNITS):
                    xl, half = u // 2, u % 2
                    dve.wait_ge(S["P"], UNITS * n + u + 1)
                    src = ps[:, u % RING].rearrange("p (h t) -> p h t", t=P)
                    dst = PM[:, half].rearrange("p k b t -> p (k b) t")
                    if xl == 0:
                        nc.vector.tensor_tensor(dst, src, mask[:, 1].unsqueeze(1).broadcast_to([P, BH, P]),
                                                ALU.mult).then_inc(S["PM"], 1)
                    else:
                        dve.wait_ge(S["PM"], UNITS * n + u - 1)
                        at = xl + 1 if xl < NL else BASE
                        nc.vector.copy_predicated(dst, mask[:, at].bitcast(U32).unsqueeze(1).broadcast_to([P, BH, P]),
                                                  src).then_inc(S["PM"], 1)
                    if u == RING and n < NC - 1:
                        dve.wait_ge(S["st"], n + 1)
                        if n:
                            dve.wait_ge(S["St"], n)
                        for rows in (slice(0, BD), slice(BD, P)):
                            new = bank_s.rearrange("p (k b t) -> p k b t", k=KC, b=B)[rows, :, :, rows]
                            if n == 0:
                                last = nc.vector.tensor_copy(St[rows, 0, :, :, rows], new)
                            else:
                                for k in range(KC):
                                    for b in range(B):
                                        last = nc.vector.scalar_tensor_tensor(
                                            St[rows, e, k, b, rows], St[rows, 1 - e, k, b, rows], F[rows, NX + 1, k, b, P - 1:P],
                                            new[:, k, b], ALU.mult, ALU.add)
                        last.then_inc(S["St"], 1)
            add(NC - 1)
            dve.wait_ge(S["x"], 2 * NC)


def mixer(nc, w, out):
    x_in = w["L0_attn_a_hidden_states"]
    with ExitStack() as ctx:
        def sb(name, shape, dt=F32):
            return ctx.enter_context(nc.sbuf_tensor(name, shape, dt))
        x = sb("x", [P, TILES, HID])
        hT = sb("hT", [P, KC, TILES * P])
        const = sb("const", [P, N_CONST])
        beta_rows = sb("beta_rows", [P, TILES, H])
        l_all = sb("l_all", [P, H, TILES])
        g_dram = nc.dram_tensor("g_scratch", [H, P, TILES, D], F32, kind="Internal").ap()
        o_dram = nc.dram_tensor("o_scratch", [TILES, P, H * D], F32, kind="Internal").ap()
        part = [const[:, p0:p1] for p0, p1 in zip(CONST_AT, CONST_AT[1:])]
        consts = {"sums": part[0].rearrange("p (l t) -> p l t", t=P), "mask": part[1].rearrange("p (l t) -> p l t", t=P),
                  "ident": part[2], "before": part[3],
                  "half": part[4].rearrange("p (l b t) -> p l b t", l=NL, b=B), "base": part[5].rearrange("p (b t) -> p b t", b=B)}
        ident = consts["ident"]

        with Phase(nc, "load") as ph:
            loaded = ph.sem("loaded")
            blk = ph.block()

            @blk.sync
            def _(sp):
                sp.dma_start(x[:], x_in.rearrange("b (n p) c -> p (b n) c", p=P)).then_inc(loaded, 16)
                sp.dma_start(const[:], w["constants"]).then_inc(loaded, 16)
                sp.wait_ge(loaded, 32)

        layer_norm(nc, "ln1", x, ident, hT)
        slot_decays(nc, hT, w, beta_rows, g_dram)
        slot_attention(nc, hT, w, consts, beta_rows, g_dram, o_dram, l_all)
        W = {"gate": sb("w_gate", [P, KC, NE]), "shared_up": sb("w_shared_up", [P, KC, 2 * SH]),
             "shared_down": sb("w_shared_down", [SH, HID]), "up": sb("w_up", [P, KC, NE, 2 * EH]),
             "down": sb("w_down", [P, NE * EH // P, HID])}
        loads = [(W[n][:], w[f"L0_ffn_w_{n}"].rearrange("(k p) n -> p k n", p=P)) for n in ("gate", "shared_up")]
        loads += [(W["shared_down"][:], w["L0_ffn_w_shared_down"])]
        loads += [(W["up"][:, k], w["L0_ffn_w_up"].rearrange("e (k p) n -> k p e n", p=P)[k]) for k in range(KC)]
        loads += [(W["down"][:], w["L0_ffn_w_down"].rearrange("e h c -> (e h) c").rearrange("(q p) c -> p q c", p=P))]
        gated_output(nc, x, hT, w, ident, o_dram, l_all, loads)
        layer_norm(nc, "ln2", x, ident, hT)
        experts(nc, "ffn1", x, hT, W, consts)
        layer_norm(nc, "ln3", x, ident, hT, w["L0_attn_b_gamma"], w["L0_attn_b_beta"])
        linear_attention(nc, x, hT, w, consts)
        layer_norm(nc, "ln4", x, ident, hT)
        experts(nc, "ffn2", x, hT, W, consts)

        with Phase(nc, "store") as ph:
            stored = ph.sem("stored")
            blk = ph.block()

            @blk.sync
            def _(sp):
                sp.dma_start(out.rearrange("b (n p) c -> p (b n) c", p=P), x[:]).then_inc(stored, 16)
                sp.wait_ge(stored, 16)


_INS = ["L0_attn_a_hidden_states", *(f"L0_attn_a_{n}" for n in (
    "Wq Wk Wv Ww cq ck cv Wf1 Wf2 Wb Wg1 Wg2 bg2 norm_w Wo").split()),
    *(f"L0_attn_b_{n}" for n in "Wx Ww bw Wk Wv Wr Wout gamma beta".split()),
    *(f"L0_ffn_{n}" for n in "w_gate w_shared_up w_shared_down w_up w_down".split())]


def kernel(**inputs):
    import numpy as _np
    import concourse.bacc as _bacc
    from concourse import mybir as _mybir
    from concourse.bass_utils import run_bass_kernel_spmd as _run

    nc = _bacc.Bacc("TRN2", target_bir_lowering=False, num_devices=1)
    arrays, w = {}, {}
    for name in _INS + ["constants"]:
        a = constants() if name == "constants" else _np.ascontiguousarray(inputs[name])
        arrays[f"in_{name}"] = a
        w[name] = nc.dram_tensor(f"in_{name}", a.shape, _mybir.dt.from_np(a.dtype), kind="ExternalInput").ap()
    out = nc.dram_tensor("out_0", (B, T, HID), F32, kind="ExternalOutput").ap()
    mixer(nc, w, out)
    r = _run(nc, [arrays], core_ids=[0])
    return r.results[0]["out_0"]
```
